# Optimizing a Trainium2 kernel written in Bass

```python
import numpy as np
import jax
import jax.numpy as jnp

def _softmax(x, axis=-1):
    return jax.nn.softmax(x, axis=axis)

def _gelu(x):
    return jax.nn.gelu(x, approximate=True)

def _silu(x):
    return jax.nn.silu(x)

def _sigmoid(x):
    return jax.nn.sigmoid(x)

def _layernorm(x, axis=-1, eps=1e-05):
    m = jnp.mean(x, axis=axis, keepdims=True)
    v = jnp.var(x, axis=axis, keepdims=True)
    return (x - m) / jnp.sqrt(v + eps)

def _scatter_add(tgt, idx, src, axis=0):
    return tgt.at[idx].add(src)

def _segment_sum(src, seg, n):
    return jax.ops.segment_sum(src, seg, n)
kernel_name = 'mk_adj_resnorm_d4_adj_r2_682173'

def setup_inputs(seed: int=0):
    np.random.seed(seed)
    _w = jnp.asarray

    def _rec_inputs():
        import jax
        import jax.numpy as jnp
        _gk = jax.random.key(seed)
        x = -0.0003929 + 0.9999 * jax.random.normal(jax.random.fold_in(_gk, 1), (32, 256, 512), jnp.float32)
        _a = jax.random.bernoulli(jax.random.fold_in(_gk, 2), 0.0625, (256, 256))
        _a = jnp.logical_or(_a, jnp.swapaxes(_a, -1, -2))
        _a = jnp.logical_or(_a, jnp.eye(256, dtype=bool))
        _af = _a.astype(jnp.float32)
        _af = _af * jax.random.uniform(jax.random.fold_in(_gk, 3), (256, 256), jnp.float32, 0.05, 0.198159)
        adj = _af
        return (x, adj)
    x, adj = _rec_inputs()

    def _L0_gnn_setup():
        import jax, jax.numpy as jnp
        import numpy as np
        NEG_SLOPE = 0.01
        key = jax.random.key(seed)
        k1, k2, k3, k4, k5 = jax.random.split(key, 5)
        B, C, N, O = (32, 256, 512, 256)
        x = jax.random.normal(k1, (B, C, N), dtype=jnp.float32)
        wq = jax.random.normal(k2, (C,), dtype=jnp.float32) * (1.0 / np.sqrt(C))
        wk = jax.random.normal(k3, (C,), dtype=jnp.float32) * (1.0 / np.sqrt(C))
        wm = jax.random.normal(k4, (O, C), dtype=jnp.float32) * (1.0 / np.sqrt(C))
        bm = jax.random.normal(k5, (O,), dtype=jnp.float32) * 0.01
        return {'x': x, 'wq': wq, 'wk': wk, 'wm': wm, 'bm': bm}
    _L0_gnn_all = _L0_gnn_setup()
    _L0_gnn_in = {k: v for k, v in _L0_gnn_all.items() if k in ('wq', 'wk', 'bm')}
    del _L0_gnn_all

    def _L1_gnn_setup():
        import jax, jax.numpy as jnp
        import numpy as np
        EPS = 1e-08

        def _row_stochastic_causal(A, causal_mask):
            A = A * causal_mask
            deg = jnp.maximum(A.sum(axis=-1, keepdims=True), EPS)
            return A / deg
        key = jax.random.key(seed)
        k = jax.random.split(key, 5)
        B, N, D = (4, 1024, 512)
        s = 1.0 / np.sqrt(D)
        h = jax.random.normal(k[0], (B, N, D), dtype=jnp.float32)
        W_lang = jax.random.normal(k[1], (D, D), dtype=jnp.float32) * s
        W_grav = jax.random.normal(k[2], (D, D), dtype=jnp.float32) * s
        W_V = jax.random.normal(k[3], (D, D), dtype=jnp.float32) * s
        W_O = jax.random.normal(k[4], (D, D), dtype=jnp.float32) * s
        causal_mask = jnp.tril(jnp.ones((N, N), dtype=jnp.float32))
        gate_logit = jnp.zeros((), jnp.float32)
        log_sigma = jnp.zeros((), jnp.float32)
        return {'h': h, 'causal_mask': causal_mask, 'W_lang': W_lang, 'W_grav': W_grav, 'W_V': W_V, 'W_O': W_O, 'gate_logit': gate_logit, 'log_sigma': log_sigma}
    _L1_gnn_all = _L1_gnn_setup()
    _L1_gnn_in = {k: v for k, v in _L1_gnn_all.items() if k in ('W_lang', 'W_grav', 'W_V', 'W_O', 'gate_logit', 'log_sigma')}
    del _L1_gnn_all

    def _L2_gnn_setup():
        import jax, jax.numpy as jnp
        import numpy as np
        DIM = 199
        K_HOP = 3

        def _khop_support(n, k):
            A = np.eye(n, dtype=np.float64)
            idx = np.arange(n)
            A[idx, (idx + 1) % n] = 1.0
            A[(idx + 1) % n, idx] = 1.0
            S = np.linalg.matrix_power(A, k)
            return (S > 0).astype(np.float32)
        key = jax.random.key(seed)
        kx, kk = jax.random.split(key)
        batch, n, f = (128, DIM, 512)
        x = jax.random.normal(kx, (batch, n, f), dtype=jnp.float32)
        support = jnp.asarray(_khop_support(n, K_HOP))
        limit = float(np.sqrt(6.0 / (n + n)))
        kernel = jax.random.uniform(kk, (n, n), minval=-limit, maxval=limit, dtype=jnp.float32)
        bias = jnp.zeros((f,), dtype=jnp.float32)
        return {'x': x, 'support': support, 'kernel': kernel, 'bias': bias}
    _L2_gnn_all = _L2_gnn_setup()
    _L2_gnn_in = {k: v for k, v in _L2_gnn_all.items() if k in ('bias',)}
    del _L2_gnn_all

    def _L3_gnn_setup():
        import jax, jax.numpy as jnp
        import numpy as np
        EPS = 1e-08

        def _row_stochastic_causal(A, causal_mask):
            A = A * causal_mask
            deg = jnp.maximum(A.sum(axis=-1, keepdims=True), EPS)
            return A / deg
        key = jax.random.key(seed)
        k = jax.random.split(key, 5)
        B, N, D = (4, 1024, 512)
        s = 1.0 / np.sqrt(D)
        h = jax.random.normal(k[0], (B, N, D), dtype=jnp.float32)
        W_lang = jax.random.normal(k[1], (D, D), dtype=jnp.float32) * s
        W_grav = jax.random.normal(k[2], (D, D), dtype=jnp.float32) * s
        W_V = jax.random.normal(k[3], (D, D), dtype=jnp.float32) * s
        W_O = jax.random.normal(k[4], (D, D), dtype=jnp.float32) * s
        causal_mask = jnp.tril(jnp.ones((N, N), dtype=jnp.float32))
        gate_logit = jnp.zeros((), jnp.float32)
        log_sigma = jnp.zeros((), jnp.float32)
        return {'h': h, 'causal_mask': causal_mask, 'W_lang': W_lang, 'W_grav': W_grav, 'W_V': W_V, 'W_O': W_O, 'gate_logit': gate_logit, 'log_sigma': log_sigma}
    _L3_gnn_all = _L3_gnn_setup()
    _L3_gnn_in = {k: v for k, v in _L3_gnn_all.items() if k in ('W_lang', 'W_grav', 'W_V', 'W_O', 'gate_logit', 'log_sigma')}
    del _L3_gnn_all
    return {'x': x, 'adj': adj, 'L0_gnn_wq': _L0_gnn_in['wq'], 'L0_gnn_wk': _L0_gnn_in['wk'], 'L0_gnn_bm': _L0_gnn_in['bm'], 'L1_gnn_W_lang': _L1_gnn_in['W_lang'], 'L1_gnn_W_grav': _L1_gnn_in['W_grav'], 'L1_gnn_W_V': _L1_gnn_in['W_V'], 'L1_gnn_W_O': _L1_gnn_in['W_O'], 'L1_gnn_gate_logit': _L1_gnn_in['gate_logit'], 'L1_gnn_log_sigma': _L1_gnn_in['log_sigma'], 'L2_gnn_bias': _L2_gnn_in['bias'], 'L3_gnn_W_lang': _L3_gnn_in['W_lang'], 'L3_gnn_W_grav': _L3_gnn_in['W_grav'], 'L3_gnn_W_V': _L3_gnn_in['W_V'], 'L3_gnn_W_O': _L3_gnn_in['W_O'], 'L3_gnn_gate_logit': _L3_gnn_in['gate_logit'], 'L3_gnn_log_sigma': _L3_gnn_in['log_sigma']}

def reference(x, adj, L0_gnn_wq, L0_gnn_wk, L0_gnn_bm, L1_gnn_W_lang, L1_gnn_W_grav, L1_gnn_W_V, L1_gnn_W_O, L1_gnn_gate_logit, L1_gnn_log_sigma, L2_gnn_bias, L3_gnn_W_lang, L3_gnn_W_grav, L3_gnn_W_V, L3_gnn_W_O, L3_gnn_gate_logit, L3_gnn_log_sigma):
    import jax
    import jax.numpy as jnp

    def _L0_gnn_ref(x, wq, wk, wm, bm):
        import jax, jax.numpy as jnp
        import numpy as np
        NEG_SLOPE = 0.01
        q = jnp.einsum('c,bcn->bn', wq, x)
        k = jnp.einsum('c,bcn->bn', wk, x)
        scores = q[:, None, :] + k[:, :, None]
        scores = jnp.where(scores > 0, scores, NEG_SLOPE * scores)
        att = jax.nn.softmax(scores, axis=-1)
        agg = jnp.einsum('bcn,bmn->bcm', x, att)
        out = jnp.einsum('oc,bcm->bom', wm, agg) + bm[None, :, None]
        return jax.nn.relu(out)

    def _L1_gnn_ref(h, causal_mask, W_lang, W_grav, W_V, W_O, gate_logit, log_sigma):
        import jax, jax.numpy as jnp
        import numpy as np
        EPS = 1e-08

        def _row_stochastic_causal(A, causal_mask):
            A = A * causal_mask
            deg = jnp.maximum(A.sum(axis=-1, keepdims=True), EPS)
            return A / deg
        z_l = jnp.einsum('bnd,ed->bne', h, W_lang)
        z_g = jnp.einsum('bnd,ed->bne', h, W_grav)
        v = jnp.einsum('bnd,ed->bne', h, W_V)
        N = h.shape[-2]
        not_eye = 1.0 - jnp.eye(N, dtype=h.dtype)
        zn = z_l / jnp.maximum(jnp.linalg.norm(z_l, axis=-1, keepdims=True), EPS)
        A_l = jnp.maximum(jnp.einsum('bnd,bmd->bnm', zn, zn), 0.0) * not_eye
        sq = jnp.sum(z_g * z_g, axis=-1, keepdims=True)
        d2 = jnp.maximum(sq + jnp.swapaxes(sq, -1, -2) - 2.0 * jnp.einsum('bnd,bmd->bnm', z_g, z_g), 0.0)
        sigma = jnp.exp(log_sigma)
        A_g = jnp.exp(-d2 / (2.0 * sigma * sigma)) * not_eye
        K_l = _row_stochastic_causal(A_l, causal_mask)
        K_g = _row_stochastic_causal(A_g, causal_mask)
        w_l = jax.nn.sigmoid(gate_logit)
        K = w_l * K_l + (1.0 - w_l) * K_g
        out = jnp.einsum('bnm,bmd->bnd', K, v)
        return jnp.einsum('bnd,ed->bne', out, W_O)

    def _L2_gnn_ref(x, support, kernel, bias):
        import jax, jax.numpy as jnp
        import numpy as np
        DIM = 199
        K_HOP = 3

        def _khop_support(n, k):
            A = np.eye(n, dtype=np.float64)
            idx = np.arange(n)
            A[idx, (idx + 1) % n] = 1.0
            A[(idx + 1) % n, idx] = 1.0
            S = np.linalg.matrix_power(A, k)
            return (S > 0).astype(np.float32)
        W = support * kernel
        out = jnp.einsum('bnf,nm->bmf', x, W)
        out = out + bias
        return out

    def _L3_gnn_ref(h, causal_mask, W_lang, W_grav, W_V, W_O, gate_logit, log_sigma):
        import jax, jax.numpy as jnp
        import numpy as np
        EPS = 1e-08

        def _row_stochastic_causal(A, causal_mask):
            A = A * causal_mask
            deg = jnp.maximum(A.sum(axis=-1, keepdims=True), EPS)
            return A / deg
        z_l = jnp.einsum('bnd,ed->bne', h, W_lang)
        z_g = jnp.einsum('bnd,ed->bne', h, W_grav)
        v = jnp.einsum('bnd,ed->bne', h, W_V)
        N = h.shape[-2]
        not_eye = 1.0 - jnp.eye(N, dtype=h.dtype)
        zn = z_l / jnp.maximum(jnp.linalg.norm(z_l, axis=-1, keepdims=True), EPS)
        A_l = jnp.maximum(jnp.einsum('bnd,bmd->bnm', zn, zn), 0.0) * not_eye
        sq = jnp.sum(z_g * z_g, axis=-1, keepdims=True)
        d2 = jnp.maximum(sq + jnp.swapaxes(sq, -1, -2) - 2.0 * jnp.einsum('bnd,bmd->bnm', z_g, z_g), 0.0)
        sigma = jnp.exp(log_sigma)
        A_g = jnp.exp(-d2 / (2.0 * sigma * sigma)) * not_eye
        K_l = _row_stochastic_causal(A_l, causal_mask)
        K_g = _row_stochastic_causal(A_g, causal_mask)
        w_l = jax.nn.sigmoid(gate_logit)
        K = w_l * K_l + (1.0 - w_l) * K_g
        out = jnp.einsum('bnm,bmd->bnd', K, v)
        return jnp.einsum('bnd,ed->bne', out, W_O)
    x = _layernorm(x + _L0_gnn_ref(x, L0_gnn_wq, L0_gnn_wk, adj, L0_gnn_bm), axis=-1)
    x = _layernorm(x + _L1_gnn_ref(x, adj, L1_gnn_W_lang, L1_gnn_W_grav, L1_gnn_W_V, L1_gnn_W_O, L1_gnn_gate_logit, L1_gnn_log_sigma), axis=-1)
    x = _layernorm(x + _L2_gnn_ref(x, adj, adj, L2_gnn_bias), axis=-1)
    x = _layernorm(x + _L3_gnn_ref(x, adj, L3_gnn_W_lang, L3_gnn_W_grav, L3_gnn_W_V, L3_gnn_W_O, L3_gnn_gate_logit, L3_gnn_log_sigma), axis=-1)
    return x

_drawn_inputs = setup_inputs


def setup_inputs(seed=0):
    import zlib

    import numpy as np

    out = dict(_drawn_inputs(seed))
    spreads = {'L2_gnn_bias': (0.0, 0.1)}
    factors = {'L0_gnn_wq': 5.608, 'L0_gnn_wk': 4.833, 'L0_gnn_bm': 200.0}
    for name, (base, spread) in spreads.items():
        noise = np.random.default_rng([zlib.crc32(name.encode()), seed]).standard_normal(out[name].shape)
        drawn = base * np.exp(spread * noise) if base else spread * noise
        out[name] = jnp.asarray(drawn.astype(out[name].dtype))
    for name, factor in factors.items():
        out[name] = (out[name] * factor).astype(out[name].dtype)
    return out
```

```python
from contextlib import ExitStack

import concourse.bass as bass
from concourse import mybir
from concourse.alu_op_type import AluOpType as ALU

F32 = mybir.dt.float32
F32R = mybir.dt.float32r
ACT = mybir.ActivationFunctionType
AX = mybir.AxisListType

P = 128
U = 512
EPS_LN = 1e-5
EPS_KERNEL = 1e-8
SLOPE = 0.01
DVE_LINKS = 23


def gnn_stack(nc, x, adj, wq, wk, bm, w1l, w1g, w1v, w1o, gate1, sigma1, bias2,
              w3l, w3g, w3v, w3o, gate3, sigma3, out):
    batches, nodes, feats = x.shape
    NT = nodes // P
    FT = feats // P
    TURNS = batches // 2
    x_tiles = x.rearrange("b (t p) n -> p (b t) n", p=P)
    out_tiles = out.rearrange("b (t p) n -> p (b t) n", p=P)

    ctx = ExitStack()
    with ctx:
        def sbuf(name, shape, dtype=F32):
            return ctx.enter_context(nc.sbuf_tensor(name, shape, dtype))

        def sem(name):
            return ctx.enter_context(nc.semaphore(name))

        def sems(name):
            return [sem(f"{name}{s}") for s in range(2)]

        ident = sbuf("ident", [P, P])
        ones = sbuf("ones", [P, P], F32R)
        adj_rhs_hi = sbuf("adj_rhs_hi", [P, NT, nodes + 2], F32R)
        adj_rhs_lo = sbuf("adj_rhs_lo", [P, NT, nodes + 2], F32R)
        adj_off = sbuf("adj_off", [P, NT, nodes])
        w2_hi = sbuf("w2_hi", [P, NT, nodes], F32R)
        w2_lo = sbuf("w2_lo", [P, NT, nodes], F32R)
        bm_col = sbuf("bm_col", [P, NT])
        bias2_row = sbuf("bias2_row", [P, U])
        minus_half = sbuf("minus_half", [P, NT])
        gate_in = sbuf("gate_in", [P, 2, 2])
        gate_tmp = sbuf("gate_tmp", [P, 2, 2])
        mix = [sbuf(f"mix{l}", [P, 2, NT]) for l in range(2)]
        inv_s2 = [sbuf(f"inv_s2{l}", [P, 1]) for l in range(2)]
        names = ("l", "g", "vo")
        w_hi = [{k: sbuf(f"w{l}{k}_hi", [P, FT, U], F32R) for k in names} for l in range(2)]
        w_lo = [{k: sbuf(f"w{l}{k}_lo", [P, FT, U], F32R) for k in names} for l in range(2)]

        full = [sbuf(f"full{s}", [P, 8, U]) for s in range(2)]
        X = [f[:, 0:2, :] for f in full]
        CUR = [f[:, 2:4, :] for f in full]
        M = [f[:, 4:8, :] for f in full]
        XS = [sbuf(f"xs{s}", [P, 4, U], F32R) for s in range(2)]
        ZS = [sbuf(f"zs{s}", [P, 8, U], F32R) for s in range(2)]
        VS = [sbuf(f"vs{s}", [P, 4, U], F32R) for s in range(2)]
        qk = [sbuf(f"qk{s}", [P, FT, 2]) for s in range(2)]
        qmax_col = [sbuf(f"qmax_col{s}", [P, 1]) for s in range(2)]
        qmax = [sbuf(f"qmax{s}", [P, 1]) for s in range(2)]
        dq = [sbuf(f"dq{s}", [P, FT]) for s in range(2)]
        a_col = [sbuf(f"a_col{s}", [P, FT]) for s in range(2)]
        b_col = [sbuf(f"b_col{s}", [P, FT]) for s in range(2)]
        ssum = [sbuf(f"ssum{s}", [P, FT]) for s in range(2)]
        rsum = [sbuf(f"rsum{s}", [P, FT]) for s in range(2)]
        stats = [sbuf(f"stats{s}", [P, NT, 6]) for s in range(2)]
        mv = [sbuf(f"mv{s}", [P, NT, 2]) for s in range(2)]
        count = [sbuf(f"count{s}", [P, 1]) for s in range(2)]
        veps = [sbuf(f"veps{s}", [P, NT]) for s in range(2)]
        rstd = [sbuf(f"rstd{s}", [P, NT]) for s in range(2)]
        diag = [sbuf(f"diag{s}", [P, 2, NT]) for s in range(2)]
        sq_l = [sbuf(f"sq_l{s}", [P, NT]) for s in range(2)]
        rnq = [sbuf(f"rnq{s}", [P, 2, NT]) for s in range(2)]
        gbias = [sbuf(f"gbias{s}", [P, NT]) for s in range(2)]
        deg = [sbuf(f"deg{s}", [P, 2, NT]) for s in range(2)]
        degm = [sbuf(f"degm{s}", [P, 2, NT]) for s in range(2)]
        rdeg = [sbuf(f"rdeg{s}", [P, 2, NT]) for s in range(2)]
        coef = [sbuf(f"coef{s}", [P, 2, NT]) for s in range(2)]
        psum = [ctx.enter_context(nc.psum_tensor(f"psum{s}", [P, 4, U], F32)) for s in range(2)]

        XH = [t[:, 0:2, :] for t in XS]
        XL = [t[:, 2:4, :] for t in XS]

        def cut(t, a, b, width):
            return t[:, a:b, :].rearrange("p a (c w) -> p (a c) w", w=width)

        HTH = [cut(t, 0, 2, nodes) for t in XS]
        HTL = [cut(t, 2, 4, nodes) for t in XS]
        YTH = [cut(t, 0, 2, nodes) for t in VS]
        YTL = [cut(t, 2, 4, nodes) for t in VS]
        VH = [t[:, 0:2, :] for t in VS]
        VL = [t[:, 2:4, :] for t in VS]
        ATH = [t[:, 0:4, :] for t in ZS]
        ATL = [t[:, 4:8, :] for t in ZS]
        ZH = [[cut(t, 4 * k, 4 * k + 2, nodes) for k in range(2)] for t in ZS]
        ZL = [[cut(t, 4 * k + 2, 4 * k + 4, nodes) for k in range(2)] for t in ZS]
        KTH = [cut(t, 0, 1, nodes) for t in ZS]
        KTL = [cut(t, 1, 2, nodes) for t in ZS]

        def plain(ap):
            return ap.bitcast(F32)

        def halves(row):
            return row.rearrange("p (t m) -> p t m", m=nodes)

        def squares(row):
            return row.rearrange("p (t m) -> p t m", m=P)

        x_loaded = sems("x_loaded")
        xh_ready = sems("xh_ready")
        xl_ready = sems("xl_ready")
        yt_done = sems("yt_done")
        yth_ready = sems("yth_ready")
        ytl_ready = sems("ytl_ready")
        kmat_ready = sems("kmat_ready")
        kb_done = sems("kb_done")
        dq_ready = sems("dq_ready")
        rows_ready = sems("rows_ready")
        cols_exp = sems("cols_exp")
        rows_exp = sems("rows_exp")
        btmp_ready = sems("btmp_ready")
        att_ready = sems("att_ready")
        ath_ready = sems("ath_ready")
        atl_ready = sems("atl_ready")
        s_done = sems("s_done")
        agg_done = sems("agg_done")
        smat_ready = sems("smat_ready")
        rb_done = sems("rb_done")
        rrow_ready = sems("rrow_ready")
        scaled_ready = sems("scaled_ready")
        relu_ready = sems("relu_ready")
        res_ready = sems("res_ready")
        stats_ready = sems("stats_ready")
        var_ready = sems("var_ready")
        rstd_ready = sems("rstd_ready")
        cur_ready = sems("cur_ready")
        ht_done = sems("ht_done")
        hth_ready = sems("hth_ready")
        htl_ready = sems("htl_ready")
        z_done = sems("z_done")
        zh_ready = sems("zh_ready")
        zl_ready = sems("zl_ready")
        gram_done = sems("gram_done")
        v_done = sems("v_done")
        vh_ready = sems("vh_ready")
        vl_ready = sems("vl_ready")
        sq_ready = sems("sq_ready")
        rn_ready = sems("rn_ready")
        mat_ready = sems("mat_ready")
        bc_done = sems("bc_done")
        sqrow_ready = sems("sqrow_ready")
        dist_ready = sems("dist_ready")
        gauss_ready = sems("gauss_ready")
        coef_ready = sems("coef_ready")
        ag_ready = sems("ag_ready")
        k_ready = sems("k_ready")
        kt_done = sems("kt_done")
        kth_ready = sems("kth_ready")
        ktl_ready = sems("ktl_ready")
        kv_done = sems("kv_done")
        x2h_ready = sems("x2h_ready")
        x2l_ready = sems("x2l_ready")
        l2_done = sems("l2_done")
        stored = sems("stored")
        dve_link = sems("dve_link")

        adj_loaded = sem("adj_loaded")
        small_loaded = sem("small_loaded")
        w_loaded = [sem(f"w_loaded{n}") for n in range(8)]
        zeros_ready = sem("zeros_ready")
        ident_ready = sem("ident_ready")
        prep_link = sem("prep_link")
        prep_pe = sem("prep_pe")
        prep_hi = sem("prep_hi")
        prep_out = sem("prep_out")
        gate_exp = sem("gate_exp")
        adj_t_done = sem("adj_t_done")
        adj_prep = sem("adj_prep")

        half = [full[0][:, 0:4, :], full[0][:, 4:8, :], full[1][:, 0:4, :], full[1][:, 4:8, :]]
        jobs = [("l", 0, half[0]), ("g", 0, half[1]), ("o", 0, half[3]), ("vo", 0, half[2]),
                ("l", 1, half[1]), ("g", 1, half[0]), ("o", 1, half[3]), ("vo", 1, half[2])]
        o_transposed = [half[0], half[1]]
        loads = [(w1l, half[0], 0), (w1g, half[1], 0), (w1v, half[2], 0), (w1o, half[3], 0),
                 (w3l, half[1], 2), (w3o, half[3], 3), (w3g, half[0], 4), (w3v, half[2], 4)]
        needs = [[0], [1], [3], [2], [4], [6], [5], [7]]
        adj_nat = half[3][:, 0, :].rearrange("p (t m) -> p t m", m=nodes)
        adj_rhs = full[1][:, 5:7, 0:nodes + 2]
        w2_full = half[3][:, 3, :].rearrange("p (t m) -> p t m", m=nodes)

        scratch = [half[3][:, 1 + t, U - P:U] for t in range(NT)]

        block = ctx.enter_context(nc.Block())

        @block.sync
        def _(sp):
            sp.dma_start(adj_nat, adj.rearrange("(t p) m -> p t m", p=P)).then_inc(adj_loaded, 16)
            for c in range(NT):
                sp.dma_start(adj_rhs[:, c, nodes:nodes + 1],
                             wq[c * P:(c + 1) * P].unsqueeze(1)).then_inc(adj_loaded, 16)
                sp.dma_start(adj_rhs[:, c, nodes + 1:nodes + 2],
                             wk[c * P:(c + 1) * P].unsqueeze(1)).then_inc(adj_loaded, 16)
            sp.dma_start(half[0], w1l.rearrange("(t p) d -> p t d", p=P)).then_inc(w_loaded[0], 16)
            for c in range(NT):
                sp.dma_start(bm_col[:, c:c + 1],
                             bm[c * P:(c + 1) * P].unsqueeze(1)).then_inc(small_loaded, 16)
            sp.dma_start(bias2_row[:], bias2.unsqueeze(0).to_broadcast([P, U])).then_inc(small_loaded, 16)
            for l, (g, sg) in enumerate(((gate1, sigma1), (gate3, sigma3))):
                sp.dma_start(gate_in[:, l, 0:1], g.unsqueeze(0).to_broadcast([P, 1])).then_inc(small_loaded, 16)
                sp.dma_start(gate_in[:, l, 1:2], sg.unsqueeze(0).to_broadcast([P, 1])).then_inc(small_loaded, 16)
            for n in range(1, 8):
                src, dst, read = loads[n]
                if n == 3:
                    sp.wait_ge(adj_prep, 1)
                if read:
                    sp.wait_ge(prep_pe, 4 * read)
                sp.dma_start(dst, src.rearrange("(t p) d -> p t d", p=P)).then_inc(w_loaded[n], 16)

            def load(s, j):
                sp.dma_start(X[s], x_tiles[:, bass.ds((j * 2 + s) * NT, NT), :]).then_inc(x_loaded[s], 16)

            def store(s, j):
                sp.wait_ge(cur_ready[s], j * 4 + 4)
                sp.dma_start(out_tiles[:, bass.ds((j * 2 + s) * NT, NT), :], CUR[s]).then_inc(stored[s], 16)

            sp.wait_ge(prep_pe, 32)
            load(0, 0)
            load(1, 0)
            with sp.Fori(0, TURNS - 1) as i:
                for s in range(2):
                    sp.wait_ge(res_ready[s], i * 8 + 2)
                    load(s, i + 1)
                store(0, i)
                store(1, i)
            for s in range(2):
                store(s, TURNS - 1)
            for s in range(2):
                sp.wait_ge(stored[s], 16 * TURNS)

        @block.tensor
        def _(pe):
            mm = nc.tensor.matmul

            def product(dst, terms):
                n = 0
                for ah, al, bh, bl in terms:
                    for a, b in ((ah, bh), (ah, bl), (al, bh)):
                        last = mm(dst, a, b, start=(n == 0), stop=(n == 3 * len(terms) - 1))
                        n += 1
                return last

            def flip(dst, src):
                return mm(dst, src, ident[:], is_transpose=True, start=True, stop=True)

            pe.wait_ge(ident_ready, 1)
            pe.wait_ge(adj_loaded, 16 * 5)
            for c in range(NT):
                for o in range(NT):
                    last = flip(psum[1][:, 3, c * nodes + o * P:c * nodes + (o + 1) * P],
                                adj_nat[:, o, c * P:(c + 1) * P])
            last.then_inc(adj_t_done, 1)
            for q, (kind, l, src) in enumerate(jobs):
                if q == 1:
                    pe.wait_ge(adj_prep, 1)
                for n in needs[q]:
                    pe.wait_ge(w_loaded[n], 16)
                if q >= 2:
                    pe.wait_ge(prep_out, 4 * (q - 1))
                if kind == "vo":
                    pe.wait_ge(prep_out, 4 * q)
                for t in range(FT):
                    dst = psum[q % 2][:, t, :]
                    for e in range(FT):
                        if kind == "vo":
                            last = mm(dst, src[:, e, t * P:(t + 1) * P], o_transposed[l][:, e, :],
                                      start=(e == 0), stop=(e == FT - 1))
                        else:
                            last = flip(dst[:, e * P:(e + 1) * P], src[:, e, t * P:(t + 1) * P])
                    last.then_inc(prep_pe, 1)

            def adj_x(s, j):
                pe.wait_ge(xh_ready[s], j + 1)
                pe.wait_ge(xl_ready[s], j + 1)
                pe.wait_ge(res_ready[s], j * 8)
                for t in range(FT):
                    cols = slice(t * P, (t + 1) * P)
                    product(psum[s][:, t, 0:nodes + 2],
                            [(XH[s][:, c, cols], XL[s][:, c, cols], adj_rhs_hi[:, c, :], adj_rhs_lo[:, c, :])
                             for c in range(NT)]).then_inc(yt_done[s], 1)

            def k_rows(s, j):
                pe.wait_ge(kmat_ready[s], j + 1)
                for t in range(FT):
                    flip(psum[s][:, 0, t * P:(t + 1) * P], squares(M[s][:, 2, :])[:, t, :])
                flip(psum[s][:, 1, 0:P], M[s][:, 3, 0:P]).then_inc(kb_done[s], 1)

            def aggregate(s, j):
                for t in range(FT):
                    pe.wait_ge(ath_ready[s], j * 4 + (t + 1))
                    pe.wait_ge(atl_ready[s], j * 4 + (t + 1))
                    first, end = t == 0, t == FT - 1
                    mm(psum[s][:, 2, :], ones[:], ATH[s][:, t, :], start=first, stop=False)
                    last = mm(psum[s][:, 2, :], ones[:], ATL[s][:, t, :], start=False, stop=end)
                    if end:
                        last.then_inc(s_done[s], 1)
                    for o, bank in enumerate((3, 0)):
                        hi, lo = (y[s][:, t, o * P:(o + 1) * P] for y in (YTH, YTL))
                        dst = psum[s][:, bank, :]
                        mm(dst, hi, ATH[s][:, t, :], start=first, stop=False)
                        mm(dst, hi, ATL[s][:, t, :], start=False, stop=False)
                        last = mm(dst, lo, ATH[s][:, t, :], start=False, stop=end)
                        if end:
                            last.then_inc(agg_done[s], 1)

            def sum_rows(s, j):
                pe.wait_ge(smat_ready[s], j + 1)
                for t in range(FT):
                    last = flip(psum[s][:, 1, t * P:(t + 1) * P], squares(M[s][:, 3, :])[:, t, :])
                last.then_inc(rb_done[s], 1)

            def transpose_x(s, j, l):
                pe.wait_ge(cur_ready[s], j * 4 + (2 * l + 1))
                for d in range(FT):
                    for n in range(NT):
                        c = (d % 2) * nodes + n * P
                        last = flip(psum[s][:, 1 + d // 2, c:c + P], CUR[s][:, n, d * P:(d + 1) * P])
                    if d % 2:
                        last.then_inc(ht_done[s], 1)

            def project(s, j, l, kind, part):
                if kind == 0 and part == 0:
                    pe.wait_ge(htl_ready[s], j * 4 + (2 * l + 2))
                bank = (3, 0, 1, 2)[2 * kind + part]
                wh, wl = w_hi[l]["lg"[kind]], w_lo[l]["lg"[kind]]
                for e in (2 * part, 2 * part + 1):
                    cols = slice(e * P, (e + 1) * P)
                    last = product(psum[s][:, bank, (e % 2) * nodes:(e % 2 + 1) * nodes],
                                   [(wh[:, d, cols], wl[:, d, cols], HTH[s][:, d, :], HTL[s][:, d, :])
                                    for d in range(FT)])
                last.then_inc(z_done[s], 1)

            def gram(s, j, l, kind):
                pe.wait_ge(zl_ready[s], j * 8 + (4 * l + 2 * kind + 2))
                zh, zl = ZH[s][kind], ZL[s][kind]
                for n in range(NT):
                    cols = slice(n * P, (n + 1) * P)
                    last = product(psum[s][:, (3, 1)[kind], n * nodes:(n + 1) * nodes],
                                   [(zh[:, e, cols], zl[:, e, cols], zh[:, e, :], zl[:, e, :])
                                    for e in range(FT)])
                last.then_inc(gram_done[s], 1)

            def values(s, j, l, n):
                cols = slice(n * P, (n + 1) * P)
                wh, wl = w_hi[l]["vo"], w_lo[l]["vo"]
                product(psum[s][:, 2 * n, :],
                        [(HTH[s][:, d, cols], HTL[s][:, d, cols], wh[:, d, :], wl[:, d, :])
                         for d in range(FT)]).then_inc(v_done[s], 1)

            def norm_rows(s, j, l):
                pe.wait_ge(mat_ready[s], j * 2 + (l + 1))
                pe.wait_ge(vl_ready[s], j * 4 + (2 * l + 1))
                for t in range(4):
                    last = flip(psum[s][:, 0, t * P:(t + 1) * P], squares(M[s][:, 2, :])[:, t, :])
                last.then_inc(bc_done[s], 1)

            def transpose_k(s, j, l):
                pe.wait_ge(k_ready[s], j * 2 + (l + 1))
                for m in range(NT):
                    for n in range(NT):
                        last = flip(psum[s][:, 3, m * nodes + n * P:m * nodes + (n + 1) * P],
                                    halves(M[s][:, 0, :])[:, n, m * P:(m + 1) * P])
                last.then_inc(kt_done[s], 1)

            def mix_values(s, j, l):
                pe.wait_ge(ktl_ready[s], j * 2 + (l + 1))
                pe.wait_ge(vl_ready[s], j * 4 + (2 * l + 2))
                for n in range(NT):
                    cols = slice(n * P, (n + 1) * P)
                    product(psum[s][:, n, :],
                            [(KTH[s][:, m, cols], KTL[s][:, m, cols], VH[s][:, m, :], VL[s][:, m, :])
                             for m in range(NT)]).then_inc(kv_done[s], 1)

            def layer2(s, j):
                pe.wait_ge(x2h_ready[s], j + 1)
                pe.wait_ge(x2l_ready[s], j + 1)
                for m in range(NT):
                    cols = slice(m * P, (m + 1) * P)
                    product(psum[s][:, 2 + m, :],
                            [(w2_hi[:, n, cols], w2_lo[:, n, cols], XH[s][:, n, :], XL[s][:, n, :])
                             for n in range(NT)]).then_inc(l2_done[s], 1)

            def first_layer(s, j):
                adj_x(s, j)
                k_rows(s, j)
                aggregate(s, j)
                sum_rows(s, j)
                transpose_x(s, j, 0)

            def middle_slot(s, js, l, r, jr):
                project(s, js, l, 0, 0)
                norm_rows(r, jr, 0)
                project(s, js, l, 0, 1)
                project(s, js, l, 1, 0)
                transpose_k(r, jr, 0)
                project(s, js, l, 1, 1)
                mix_values(r, jr, 0)
                gram(s, js, l, 0)
                values(s, js, l, 0)
                layer2(r, jr)
                gram(s, js, l, 1)
                values(s, js, l, 1)
                transpose_x(r, jr, 1)

            def seam_slot(s, js, l, r, jr, jn):
                project(s, js, l, 0, 0)
                if jr is not None:
                    norm_rows(r, jr, 1)
                project(s, js, l, 0, 1)
                project(s, js, l, 1, 0)
                if jr is not None:
                    transpose_k(r, jr, 1)
                project(s, js, l, 1, 1)
                if jr is not None:
                    mix_values(r, jr, 1)
                gram(s, js, l, 0)
                if jn is not None:
                    adj_x(r, jn)
                values(s, js, l, 0)
                if jn is not None:
                    k_rows(r, jn)
                gram(s, js, l, 1)
                values(s, js, l, 1)
                if jn is not None:
                    aggregate(r, jn)
                    sum_rows(r, jn)
                    transpose_x(r, jn, 0)

            def tail(r, j):
                norm_rows(r, j, 1)
                transpose_k(r, j, 1)
                mix_values(r, j, 1)

            first_layer(0, 0)
            seam_slot(0, 0, 0, 1, None, 0)
            with pe.Fori(0, TURNS - 1) as i:
                middle_slot(1, i, 0, 0, i)
                middle_slot(0, i, 1, 1, i)
                seam_slot(1, i, 1, 0, i, i + 1)
                seam_slot(0, i + 1, 0, 1, i, i + 1)
            e = TURNS - 1
            middle_slot(1, e, 0, 0, e)
            middle_slot(0, e, 1, 1, e)
            seam_slot(1, e, 1, 0, e, None)
            tail(1, e)

        @block.scalar
        def _(act):
            def run(dst, src, func=ACT.Copy, **kw):
                return nc.scalar.activation(dst, src, func, **kw)

            act.wait_ge(small_loaded, 16 * 7)
            for l in range(2):
                run(gate_tmp[:, l, 0:1], gate_in[:, l, 0:1], ACT.Exp, scale=-1.0).then_inc(gate_exp, 1)
                run(inv_s2[l][:], gate_in[:, l, 1:2], ACT.Exp, scale=-2.0).then_inc(gate_exp, 1)
            for q, (kind, l, _) in enumerate(jobs):
                if kind == "o":
                    continue
                for t in range(FT):
                    act.wait_ge(prep_pe, 4 * q + t + 1)
                    run(w_hi[l][kind][:, t, :], psum[q % 2][:, t, :]).then_inc(prep_hi, 1)

            def split_x(s, j):
                act.wait_ge(x_loaded[s], j * 16 + 16)
                act.wait_ge(v_done[s], j * 4)
                run(XH[s], X[s]).then_inc(xh_ready[s], 1)

            def split_adj_x(s, j):
                act.wait_ge(kv_done[s], j * 4)
                for t in range(FT):
                    act.wait_ge(yt_done[s], j * 4 + (t + 1))
                    run(YTH[s][:, t, :], psum[s][:, t, 0:nodes]).then_inc(yth_ready[s], 1)

            def softmax_factors(s, j):
                act.wait_ge(dq_ready[s], j + 1)
                run(a_col[s][:], dq[s][:], ACT.Exp)
                run(b_col[s][:], dq[s][:], ACT.Exp, scale=SLOPE).then_inc(cols_exp[s], 1)
                act.wait_ge(rows_ready[s], j + 1)
                run(CUR[s][:, 1, :], CUR[s][:, 1, :], ACT.Exp, scale=SLOPE - 1.0)
                run(CUR[s][:, 0, :], CUR[s][:, 0, :], ACT.Exp, scale=1.0 - SLOPE).then_inc(rows_exp[s], 1)
                act.wait_ge(cols_exp[s], j + 1)
                act.wait_ge(rows_exp[s], j + 1)
                for t in range(FT):
                    run(M[s][:, t, :], CUR[s][:, 1, :],
                        scale=b_col[s][:, t:t + 1]).then_inc(btmp_ready[s], 1)

            def split_att(s, j):
                for t in range(FT):
                    act.wait_ge(att_ready[s], j * 4 + (t + 1))
                    run(ATH[s][:, t, :], M[s][:, t, :]).then_inc(ath_ready[s], 1)

            def sum_row(s, j):
                act.wait_ge(rb_done[s], j + 1)
                run(M[s][:, 0, :], psum[s][:, 1, :]).then_inc(rrow_ready[s], 1)

            def relu_rows(s, j):
                for o in range(NT):
                    act.wait_ge(scaled_ready[s], j * 2 + (o + 1))
                    run(M[s][:, 1 + o, :], M[s][:, 1 + o, :], ACT.Relu,
                        bias=bm_col[:, o:o + 1]).then_inc(relu_ready[s], 1)

            def split_xt(s, j, l):
                for h in range(2):
                    act.wait_ge(ht_done[s], j * 4 + (2 * l + h + 1))
                    run(XH[s][:, h, :], psum[s][:, 1 + h, :]).then_inc(hth_ready[s], 1)

            def split_z(s, j, l, kind, part):
                act.wait_ge(z_done[s], j * 8 + (4 * l + 2 * kind + part + 1))
                run(ZS[s][:, 4 * kind + part, :],
                    psum[s][:, (3, 0, 1, 2)[2 * kind + part], :]).then_inc(zh_ready[s], 1)

            def split_v(s, j, l, n):
                act.wait_ge(v_done[s], j * 4 + (2 * l + n + 1))
                run(VH[s][:, n, :], psum[s][:, 2 * n, :]).then_inc(vh_ready[s], 1)

            def sq_row(s, j, l):
                act.wait_ge(bc_done[s], j * 2 + (l + 1))
                run(M[s][:, 3, 0:nodes], psum[s][:, 0, nodes:2 * nodes]).then_inc(sqrow_ready[s], 1)

            def gauss(s, j, l):
                act.wait_ge(dist_ready[s], j * 2 + (l + 1))
                m = halves(M[s][:, 1, :])
                for n in range(NT):
                    last = run(m[:, n, :], m[:, n, :], ACT.Exp, scale=inv_s2[l][:], bias=gbias[s][:, n:n + 1])
                last.then_inc(gauss_ready[s], 1)

            def weigh_gauss(s, j, l):
                act.wait_ge(coef_ready[s], j * 2 + (l + 1))
                m = halves(M[s][:, 1, :])
                for n in range(NT):
                    last = run(m[:, n, :], m[:, n, :], scale=coef[s][:, 1, n:n + 1])
                last.then_inc(ag_ready[s], 1)

            def split_kt(s, j, l):
                act.wait_ge(kt_done[s], j * 2 + (l + 1))
                run(ZS[s][:, 0, :], psum[s][:, 3, :]).then_inc(kth_ready[s], 1)

            def split_x2(s, j):
                act.wait_ge(cur_ready[s], j * 4 + 2)
                run(XH[s], CUR[s]).then_inc(x2h_ready[s], 1)

            def first_layer(s, j):
                split_x(s, j)
                split_adj_x(s, j)
                softmax_factors(s, j)
                split_att(s, j)
                sum_row(s, j)
                relu_rows(s, j)
                split_xt(s, j, 0)

            def middle_slot(s, js, l, r, jr):
                split_z(s, js, l, 0, 0)
                sq_row(r, jr, 0)
                gauss(r, jr, 0)
                split_z(s, js, l, 0, 1)
                weigh_gauss(r, jr, 0)
                split_z(s, js, l, 1, 0)
                split_kt(r, jr, 0)
                split_z(s, js, l, 1, 1)
                split_v(s, js, l, 0)
                split_x2(r, jr)
                split_v(s, js, l, 1)
                split_xt(r, jr, 1)

            def seam_slot(s, js, l, r, jr, jn):
                split_z(s, js, l, 0, 0)
                if jr is not None:
                    sq_row(r, jr, 1)
                    gauss(r, jr, 1)
                split_z(s, js, l, 0, 1)
                if jr is not None:
                    weigh_gauss(r, jr, 1)
                if jn is not None:
                    split_x(r, jn)
                split_z(s, js, l, 1, 0)
                if jr is not None:
                    split_kt(r, jr, 1)
                split_z(s, js, l, 1, 1)
                if jn is not None:
                    split_adj_x(r, jn)
                split_v(s, js, l, 0)
                if jn is not None:
                    softmax_factors(r, jn)
                split_v(s, js, l, 1)
                if jn is not None:
                    split_att(r, jn)
                    sum_row(r, jn)
                    relu_rows(r, jn)
                    split_xt(r, jn, 0)

            def tail(r, j):
                sq_row(r, j, 1)
                gauss(r, j, 1)
                weigh_gauss(r, j, 1)
                split_kt(r, j, 1)

            first_layer(0, 0)
            seam_slot(0, 0, 0, 1, None, 0)
            with act.Fori(0, TURNS - 1) as i:
                middle_slot(1, i, 0, 0, i)
                middle_slot(0, i, 1, 1, i)
                seam_slot(1, i, 1, 0, i, i + 1)
                seam_slot(0, i + 1, 0, 1, i, i + 1)
            e = TURNS - 1
            middle_slot(1, e, 0, 0, e)
            middle_slot(0, e, 1, 1, e)
            seam_slot(1, e, 1, 0, e, None)
            tail(1, e)

        @block.vector
        def _(dve):
            tt = nc.vector.tensor_tensor
            ts = nc.vector.tensor_scalar
            stt = nc.vector.scalar_tensor_tensor

            links = [0, 0]

            def own(s, j, ins):
                links[s] += 1
                ins.then_inc(dve_link[s], 1)
                dve.wait_ge(dve_link[s], j * DVE_LINKS + links[s])

            def low(dst, src, hi):
                return tt(dst, src, plain(hi), ALU.subtract)

            prep = [0]

            def link(ins):
                prep[0] += 1
                ins.then_inc(prep_link, 1)
                dve.wait_ge(prep_link, prep[0])

            nc.vector.memset(minus_half[:], -0.5)
            link(nc.vector.memset(scratch[0], 1.0))
            nc.vector.tensor_copy(ones[:], scratch[0])
            dve.wait_ge(adj_loaded, 16 * 5)
            dve.wait_ge(ident_ready, 1)
            dve.wait_ge(adj_t_done, 1)
            nc.vector.tensor_copy(adj_rhs[:, :, 0:nodes],
                                  psum[1][:, 3, :].rearrange("p (t m) -> p t m", m=nodes))
            nc.vector.tensor_copy(adj_off[:], adj_nat)
            link(tt(w2_full, adj_nat, adj_nat, ALU.mult))
            for t in range(NT):
                blk = slice(t * P, (t + 1) * P)
                tt(w2_full[:, t, blk], w2_full[:, t, blk], ident[:], ALU.add)
                link(tt(scratch[t], adj_nat[:, t, blk], ident[:], ALU.mult))
                link(tt(adj_off[:, t, blk], adj_nat[:, t, blk], scratch[t], ALU.subtract))
            nc.vector.tensor_copy(adj_rhs_hi[:], adj_rhs)
            link(nc.vector.tensor_copy(w2_hi[:], w2_full))
            low(adj_rhs_lo[:], adj_rhs, adj_rhs_hi[:])
            low(w2_lo[:], w2_full, w2_hi[:]).then_inc(adj_prep, 1)
            dve.wait_ge(gate_exp, 4)
            for l in range(2):
                link(ts(gate_tmp[:, l, 1:2], gate_tmp[:, l, 0:1], 1.0, None, ALU.add))
                link(nc.vector.reciprocal(mix[l][:, 0, 0:1], gate_tmp[:, l, 1:2]))
                nc.vector.tensor_copy(mix[l][:, 0, 1:2], mix[l][:, 0, 0:1])
                for n in range(NT):
                    link(ts(mix[l][:, 1, n:n + 1], mix[l][:, 0, 0:1], -1.0, 1.0, ALU.mult, ALU.add))
            hi = 0
            for q, (kind, l, _) in enumerate(jobs):
                for t in range(FT):
                    src = psum[q % 2][:, t, :]
                    if kind == "o":
                        dve.wait_ge(prep_pe, 4 * q + t + 1)
                        nc.vector.tensor_copy(o_transposed[l][:, t, :], src).then_inc(prep_out, 1)
                    else:
                        hi += 1
                        dve.wait_ge(prep_hi, hi)
                        low(w_lo[l][kind][:, t, :], src, w_hi[l][kind][:, t, :]).then_inc(prep_out, 1)

            def norm_stats(s, j, layer):
                dve.wait_ge(res_ready[s], j * 8 + (2 * layer + 2))
                for n in range(NT):
                    ins = nc.vector.bn_stats(stats[s][:, n, :], CUR[s][:, n, :])
                ins.then_inc(stats_ready[s], 1)
                dve.wait_ge(stats_ready[s], j * 4 + (layer + 1))
                nc.vector.tensor_copy(count[s][:], stats[s][:, 0, 0:1])
                for n in range(NT):
                    ins = nc.vector.bn_aggr(mv[s][:, n, :], stats[s][:, n, :])
                own(s, j, ins)
                ts(veps[s][:], mv[s][:, :, 1], EPS_LN, None, ALU.add).then_inc(var_ready[s], 1)

            def normalise(s, j, layer):
                dve.wait_ge(rstd_ready[s], j * 4 + (layer + 1))
                for n in range(NT):
                    ins = ts(CUR[s][:, n, :], CUR[s][:, n, :], mv[s][:, n, 0:1], rstd[s][:, n:n + 1],
                             ALU.subtract, ALU.mult)
                ins.then_inc(cur_ready[s], 1)

            def split_adj_x(s, j):
                for t in range(FT):
                    dve.wait_ge(yth_ready[s], j * 4 + (t + 1))
                    low(YTL[s][:, t, :], psum[s][:, t, 0:nodes], YTH[s][:, t, :]).then_inc(ytl_ready[s], 1)
                own(s, j, nc.vector.tensor_copy(qk[s][:], psum[s][:, :, nodes:nodes + 2]))
                own(s, j, nc.vector.reduce_max(qmax_col[s][:], qk[s][:, :, 0], AX.X))
                nc.vector.tensor_copy(squares(M[s][:, 2, :]), qk[s][:, :, 1:2].to_broadcast([P, FT, P]))
                nc.vector.tensor_copy(M[s][:, 3, 0:P],
                                      qmax_col[s][:].to_broadcast([P, P])).then_inc(kmat_ready[s], 1)

            def softmax_args(s, j):
                dve.wait_ge(kb_done[s], j + 1)
                own(s, j, nc.vector.reduce_max(qmax[s][:], psum[s][:, 1, 0:P], AX.X))
                ts(dq[s][:], qk[s][:, :, 0], qmax[s][:], None, ALU.subtract).then_inc(dq_ready[s], 1)
                dve.wait_ge(stored[s], j * 16)
                ts(CUR[s][:, 1, :], psum[s][:, 0, :], qmax[s][:], 0.0, ALU.add, ALU.max)
                ts(CUR[s][:, 0, :], psum[s][:, 0, :], qmax[s][:], 0.0, ALU.add,
                   ALU.min).then_inc(rows_ready[s], 1)

            def attention(s, j):
                for t in range(FT):
                    dve.wait_ge(btmp_ready[s], j * 4 + (t + 1))
                    stt(M[s][:, t, :], CUR[s][:, 0, :], a_col[s][:, t:t + 1], M[s][:, t, :],
                        ALU.mult, ALU.max).then_inc(att_ready[s], 1)

            def sum_squares(s, j):
                dve.wait_ge(s_done[s], j + 1)
                for t in range(FT):
                    ins = nc.vector.tensor_tensor_reduce(
                        squares(M[s][:, 3, :])[:, t, :], psum[s][:, 2, t * P:(t + 1) * P], ident[:], 1.0, 0.0,
                        ALU.mult, ALU.add, ssum[s][:, t:t + 1])
                own(s, j, ins)
                own(s, j, nc.vector.reciprocal(rsum[s][:], ssum[s][:]))
                nc.vector.tensor_copy(squares(M[s][:, 3, :]),
                                      rsum[s][:].unsqueeze(2).to_broadcast([P, FT, P])).then_inc(smat_ready[s], 1)

            def scale_agg(s, j):
                dve.wait_ge(rrow_ready[s], j + 1)
                for o, bank in enumerate((3, 0)):
                    dve.wait_ge(agg_done[s], j * 2 + (o + 1))
                    tt(M[s][:, 1 + o, :], psum[s][:, bank, :], M[s][:, 0, :],
                       ALU.mult).then_inc(scaled_ready[s], 1)

            def add_x(s, j):
                for o in range(NT):
                    dve.wait_ge(relu_ready[s], j * 2 + (o + 1))
                    ins = tt(CUR[s][:, o, :], M[s][:, 1 + o, :], X[s][:, o, :], ALU.add)
                    ins.then_inc(res_ready[s], 1)

            def split_xt(s, j, l):
                for h in range(2):
                    dve.wait_ge(hth_ready[s], j * 4 + (2 * l + h + 1))
                    low(XL[s][:, h, :], psum[s][:, 1 + h, :], XH[s][:, h, :]).then_inc(htl_ready[s], 1)

            def split_z(s, j, l, kind, part):
                dve.wait_ge(zh_ready[s], j * 8 + (4 * l + 2 * kind + part + 1))
                low(ZS[s][:, 4 * kind + 2 + part, :], psum[s][:, (3, 0, 1, 2)[2 * kind + part], :],
                    ZS[s][:, 4 * kind + part, :]).then_inc(zl_ready[s], 1)

            def split_v(s, j, l, n):
                dve.wait_ge(vh_ready[s], j * 4 + (2 * l + n + 1))
                low(VL[s][:, n, :], psum[s][:, 2 * n, :], VH[s][:, n, :]).then_inc(vl_ready[s], 1)

            def cosine_start(s, j, l):
                dve.wait_ge(gram_done[s], j * 4 + (2 * l + 1))
                for n in range(NT):
                    nc.vector.tensor_tensor_reduce(
                        squares(M[s][:, 2, :])[:, n, :], psum[s][:, 3, n * (nodes + P):n * (nodes + P) + P], ident[:],
                        1.0, 0.0, ALU.mult, ALU.add, diag[s][:, 0, n:n + 1])
                own(s, j, stt(halves(M[s][:, 0, :]), halves(psum[s][:, 3, :]), 0.0, adj_off[:],
                              ALU.max, ALU.mult))
                ts(sq_l[s][:], diag[s][:, 0, :], EPS_KERNEL ** 2, None, ALU.max)

            def gauss_start(s, j, l):
                dve.wait_ge(gram_done[s], j * 4 + (2 * l + 2))
                for n in range(NT):
                    ins = nc.vector.tensor_tensor_reduce(
                        squares(M[s][:, 2, :])[:, 2 + n, :], psum[s][:, 1, n * (nodes + P):n * (nodes + P) + P], ident[:],
                        1.0, 0.0, ALU.mult, ALU.add, diag[s][:, 1, n:n + 1])
                own(s, j, ins)
                own(s, j, ts(rnq[s][:, 1, :], diag[s][:, 1, :], -0.5, None, ALU.mult))
                ts(gbias[s][:], rnq[s][:, 1, :], inv_s2[l][:], None, ALU.mult).then_inc(sq_ready[s], 1)

            def norm_squares(s, j, l):
                dve.wait_ge(rn_ready[s], j * 2 + (l + 1))
                nc.vector.tensor_copy(
                    squares(M[s][:, 2, :]),
                    rnq[s][:].rearrange("p a b -> p (a b)").unsqueeze(2).to_broadcast([P, 4, P])
                ).then_inc(mat_ready[s], 1)

            def kernel_rows(s, j, l):
                dve.wait_ge(sqrow_ready[s], j * 2 + (l + 1))
                tt(halves(M[s][:, 1, :]), halves(psum[s][:, 1, :]),
                   M[s][:, 3:4, 0:nodes].to_broadcast([P, NT, nodes]), ALU.add).then_inc(dist_ready[s], 1)
                m = halves(M[s][:, 0, :])
                for n in range(NT):
                    ins = stt(m[:, n, :], psum[s][:, 0, 0:nodes], rnq[s][:, 0, n:n + 1], m[:, n, :],
                              ALU.mult, ALU.mult, accum_out=deg[s][:, 0, n:n + 1])
                own(s, j, ins)

            def kernel_mix(s, j, l):
                dve.wait_ge(gauss_ready[s], j * 2 + (l + 1))
                g = halves(M[s][:, 1, :])
                for n in range(NT):
                    ins = stt(g[:, n, :], g[:, n, :], 1.0, adj_off[:, n, :], ALU.min, ALU.mult,
                              accum_out=deg[s][:, 1, n:n + 1])
                own(s, j, ins)
                own(s, j, ts(degm[s][:], deg[s][:], EPS_KERNEL, None, ALU.max))
                own(s, j, nc.vector.reciprocal(rdeg[s][:], degm[s][:]))
                tt(coef[s][:], rdeg[s][:], mix[l][:], ALU.mult).then_inc(coef_ready[s], 1)
                dve.wait_ge(coef_ready[s], j * 2 + (l + 1))
                dve.wait_ge(ag_ready[s], j * 2 + (l + 1))
                m = halves(M[s][:, 0, :])
                for n in range(NT):
                    ins = stt(m[:, n, :], m[:, n, :], coef[s][:, 0, n:n + 1], g[:, n, :], ALU.mult, ALU.add)
                ins.then_inc(k_ready[s], 1)

            def split_kt(s, j, l):
                dve.wait_ge(kth_ready[s], j * 2 + (l + 1))
                low(ZS[s][:, 1, :], psum[s][:, 3, :], ZS[s][:, 0, :]).then_inc(ktl_ready[s], 1)

            def add_kv(s, j, l):
                for n in range(NT):
                    dve.wait_ge(kv_done[s], j * 4 + (2 * l + n + 1))
                    tt(CUR[s][:, n, :], psum[s][:, n, :], CUR[s][:, n, :], ALU.add).then_inc(res_ready[s], 1)

            def split_x2(s, j):
                dve.wait_ge(x2h_ready[s], j + 1)
                low(XL[s], CUR[s], XH[s]).then_inc(x2l_ready[s], 1)

            def add_bias2(s, j):
                for m in range(NT):
                    dve.wait_ge(l2_done[s], j * 2 + (m + 1))
                    tt(CUR[s][:, m, :], psum[s][:, 2 + m, :], bias2_row[:], ALU.add).then_inc(res_ready[s], 1)

            def first_layer(s, j):
                split_adj_x(s, j)
                softmax_args(s, j)
                attention(s, j)
                sum_squares(s, j)
                scale_agg(s, j)
                add_x(s, j)
                norm_stats(s, j, 0)
                normalise(s, j, 0)
                split_xt(s, j, 0)

            def middle_slot(s, js, l, r, jr):
                norm_squares(r, jr, 0)
                split_z(s, js, l, 0, 0)
                kernel_rows(r, jr, 0)
                kernel_mix(r, jr, 0)
                split_z(s, js, l, 0, 1)
                split_z(s, js, l, 1, 0)
                split_kt(r, jr, 0)
                split_z(s, js, l, 1, 1)
                add_kv(r, jr, 0)
                norm_stats(r, jr, 1)
                normalise(r, jr, 1)
                split_x2(r, jr)
                cosine_start(s, js, l)
                split_v(s, js, l, 0)
                add_bias2(r, jr)
                norm_stats(r, jr, 2)
                normalise(r, jr, 2)
                gauss_start(s, js, l)
                split_v(s, js, l, 1)
                split_xt(r, jr, 1)

            def seam_slot(s, js, l, r, jr, jn):
                if jr is not None:
                    norm_squares(r, jr, 1)
                split_z(s, js, l, 0, 0)
                if jr is not None:
                    kernel_rows(r, jr, 1)
                    kernel_mix(r, jr, 1)
                split_z(s, js, l, 0, 1)
                split_z(s, js, l, 1, 0)
                if jr is not None:
                    split_kt(r, jr, 1)
                split_z(s, js, l, 1, 1)
                if jr is not None:
                    add_kv(r, jr, 1)
                    norm_stats(r, jr, 3)
                    normalise(r, jr, 3)
                    assert links[r] in (0, DVE_LINKS), links
                    links[r] = 0
                if jn is not None:
                    split_adj_x(r, jn)
                cosine_start(s, js, l)
                split_v(s, js, l, 0)
                if jn is not None:
                    softmax_args(r, jn)
                gauss_start(s, js, l)
                if jn is not None:
                    attention(r, jn)
                split_v(s, js, l, 1)
                if jn is not None:
                    sum_squares(r, jn)
                    scale_agg(r, jn)
                    add_x(r, jn)
                    norm_stats(r, jn, 0)
                    normalise(r, jn, 0)
                    split_xt(r, jn, 0)

            def tail(r, j):
                norm_squares(r, j, 1)
                kernel_rows(r, j, 1)
                kernel_mix(r, j, 1)
                split_kt(r, j, 1)
                add_kv(r, j, 1)
                norm_stats(r, j, 3)
                normalise(r, j, 3)

            first_layer(0, 0)
            seam_slot(0, 0, 0, 1, None, 0)
            with dve.Fori(0, TURNS - 1) as i:
                middle_slot(1, i, 0, 0, i)
                middle_slot(0, i, 1, 1, i)
                seam_slot(1, i, 1, 0, i, i + 1)
                seam_slot(0, i + 1, 0, 1, i, i + 1)
            e = TURNS - 1
            middle_slot(1, e, 0, 0, e)
            middle_slot(0, e, 1, 1, e)
            seam_slot(1, e, 1, 0, e, None)
            tail(1, e)

        @block.gpsimd
        def _(pool):
            nc.gpsimd.memset(ident[:], 0.0).then_inc(zeros_ready, 1)
            pool.wait_ge(zeros_ready, 1)
            nc.gpsimd.affine_select(out=ident[:], in_=ident[:], compare_op=ALU.not_equal, fill=1.0, base=0,
                                    pattern=[[-1, P]], channel_multiplier=1).then_inc(ident_ready, 1)

            def split_x(s, j):
                pool.wait_ge(xh_ready[s], j + 1)
                nc.gpsimd.tensor_tensor(XL[s], X[s], plain(XH[s]), ALU.subtract).then_inc(xl_ready[s], 1)

            def split_att(s, j):
                for t in range(FT):
                    pool.wait_ge(ath_ready[s], j * 4 + (t + 1))
                    nc.gpsimd.tensor_tensor(ATL[s][:, t, :], M[s][:, t, :], plain(ATH[s][:, t, :]),
                                            ALU.subtract).then_inc(atl_ready[s], 1)

            def inverse_std(s, j, layer):
                pool.wait_ge(var_ready[s], j * 4 + (layer + 1))
                nc.gpsimd.tensor_tensor(rstd[s][:], veps[s][:], minus_half[:], ALU.pow).then_inc(rstd_ready[s], 1)

            def inverse_norm(s, j, l):
                pool.wait_ge(sq_ready[s], j * 2 + (l + 1))
                nc.gpsimd.tensor_tensor(rnq[s][:, 0, :], sq_l[s][:], minus_half[:],
                                        ALU.pow).then_inc(rn_ready[s], 1)

            def middle_slot(s, js, l, r, jr):
                inverse_std(r, jr, 1)
                inverse_std(r, jr, 2)
                inverse_norm(s, js, l)

            def seam_slot(s, js, l, r, jr, jn):
                if jn is not None:
                    split_x(r, jn)
                if jr is not None:
                    inverse_std(r, jr, 3)
                inverse_norm(s, js, l)
                if jn is not None:
                    split_att(r, jn)
                    inverse_std(r, jn, 0)

            split_x(0, 0)
            split_att(0, 0)
            inverse_std(0, 0, 0)
            seam_slot(0, 0, 0, 1, None, 0)
            with pool.Fori(0, TURNS - 1) as i:
                middle_slot(1, i, 0, 0, i)
                middle_slot(0, i, 1, 1, i)
                seam_slot(1, i, 1, 0, i, i + 1)
                seam_slot(0, i + 1, 0, 1, i, i + 1)
            e = TURNS - 1
            middle_slot(1, e, 0, 0, e)
            middle_slot(0, e, 1, 1, e)
            seam_slot(1, e, 1, 0, e, None)
            inverse_std(1, e, 3)


_INS = ["x", "adj", "L0_gnn_wq", "L0_gnn_wk", "L0_gnn_bm",
        "L1_gnn_W_lang", "L1_gnn_W_grav", "L1_gnn_W_V", "L1_gnn_W_O", "L1_gnn_gate_logit", "L1_gnn_log_sigma",
        "L2_gnn_bias",
        "L3_gnn_W_lang", "L3_gnn_W_grav", "L3_gnn_W_V", "L3_gnn_W_O", "L3_gnn_gate_logit", "L3_gnn_log_sigma"]
_OUTS = [((32, 256, 512), "float32")]


def kernel(**inputs):
    import numpy as _np
    import concourse.bacc as _bacc
    from concourse import mybir as _mybir
    from concourse.bass_utils import run_bass_kernel_spmd as _run

    nc = _bacc.Bacc("TRN2", target_bir_lowering=False, num_devices=1)
    arrays, args = {}, []
    for name in _INS:
        a = _np.ascontiguousarray(inputs[name])
        if a.ndim == 0:
            a = a.reshape(1)
        arrays[f"in_{name}_dram"] = a
        args.append(nc.dram_tensor(f"in_{name}_dram", a.shape, _mybir.dt.from_np(a.dtype), kind="ExternalInput").ap())
    for i, (shape, dtype) in enumerate(_OUTS):
        dt = _mybir.dt.from_np(_np.dtype(dtype))
        args.append(nc.dram_tensor(f"out_{i}_dram", shape, dt, kind="ExternalOutput").ap())
    gnn_stack(nc, *args)
    r = _run(nc, [arrays], core_ids=[0])
    return r.results[0]["out_0_dram"]
```

```python
from contextlib import ExitStack

import concourse.bass as bass
from concourse import mybir
from concourse.alu_op_type import AluOpType as ALU

F32 = mybir.dt.float32
F32R = mybir.dt.float32r
ACT = mybir.ActivationFunctionType
AX = mybir.AxisListType

P = 128
U = 512
EPS_LN = 1e-5
EPS_KERNEL = 1e-8
SLOPE = 0.01
DVE_LINKS = 22


def gnn_stack(nc, x, adj, wq, wk, bm, w1l, w1g, w1v, w1o, gate1, sigma1, bias2,
              w3l, w3g, w3v, w3o, gate3, sigma3, out):
    batches, nodes, feats = x.shape
    NT = nodes // P
    FT = feats // P
    TURNS = batches // 2
    x_tiles = x.rearrange("b (t p) n -> p (b t) n", p=P)
    out_tiles = out.rearrange("b (t p) n -> p (b t) n", p=P)

    ctx = ExitStack()
    with ctx:
        def sbuf(name, shape, dtype=F32):
            return ctx.enter_context(nc.sbuf_tensor(name, shape, dtype))

        def sem(name):
            return ctx.enter_context(nc.semaphore(name))

        def sems(name):
            return [sem(f"{name}{s}") for s in range(2)]

        ident = sbuf("ident", [P, P])
        ones = sbuf("ones", [P, 1])
        adj_rhs_hi = sbuf("adj_rhs_hi", [P, NT, nodes + 2], F32R)
        adj_rhs_lo = sbuf("adj_rhs_lo", [P, NT, nodes + 2], F32R)
        adj_off = sbuf("adj_off", [P, NT, nodes])
        w2_hi = sbuf("w2_hi", [P, NT, nodes], F32R)
        w2_lo = sbuf("w2_lo", [P, NT, nodes], F32R)
        bm_col = sbuf("bm_col", [P, NT])
        bias2_row = sbuf("bias2_row", [P, U])
        minus_half = sbuf("minus_half", [P, NT])
        gate_in = sbuf("gate_in", [P, 2, 2])
        gate_tmp = sbuf("gate_tmp", [P, 2, 2])
        mix = [sbuf(f"mix{l}", [P, 2, NT]) for l in range(2)]
        inv_s2 = [sbuf(f"inv_s2{l}", [P, 1]) for l in range(2)]
        names = ("l", "g", "vo")
        w_hi = [{k: sbuf(f"w{l}{k}_hi", [P, FT, U], F32R) for k in names} for l in range(2)]
        w_lo = [{k: sbuf(f"w{l}{k}_lo", [P, FT, U], F32R) for k in names} for l in range(2)]

        full = [sbuf(f"full{s}", [P, 8, U]) for s in range(2)]
        X = [f[:, 0:2, :] for f in full]
        CUR = [f[:, 2:4, :] for f in full]
        M = [f[:, 4:8, :] for f in full]
        XS = [sbuf(f"xs{s}", [P, 4, U], F32R) for s in range(2)]
        ZS = [sbuf(f"zs{s}", [P, 8, U], F32R) for s in range(2)]
        VS = [sbuf(f"vs{s}", [P, 4, U], F32R) for s in range(2)]
        qk = [sbuf(f"qk{s}", [P, FT, 2]) for s in range(2)]
        qmax_col = [sbuf(f"qmax_col{s}", [P, 1]) for s in range(2)]
        qmax = [sbuf(f"qmax{s}", [P, 1]) for s in range(2)]
        dq = [sbuf(f"dq{s}", [P, FT]) for s in range(2)]
        a_col = [sbuf(f"a_col{s}", [P, FT]) for s in range(2)]
        b_col = [sbuf(f"b_col{s}", [P, FT]) for s in range(2)]
        rsum = [sbuf(f"rsum{s}", [P, FT]) for s in range(2)]
        stats = [sbuf(f"stats{s}", [P, NT, 6]) for s in range(2)]
        mv = [sbuf(f"mv{s}", [P, NT, 2]) for s in range(2)]
        count = [sbuf(f"count{s}", [P, 1]) for s in range(2)]
        veps = [sbuf(f"veps{s}", [P, NT]) for s in range(2)]
        rstd = [sbuf(f"rstd{s}", [P, NT]) for s in range(2)]
        diag = [sbuf(f"diag{s}", [P, 2, NT]) for s in range(2)]
        sq_l = [sbuf(f"sq_l{s}", [P, NT]) for s in range(2)]
        rnq = [sbuf(f"rnq{s}", [P, 2, NT]) for s in range(2)]
        gbias = [sbuf(f"gbias{s}", [P, NT]) for s in range(2)]
        deg = [sbuf(f"deg{s}", [P, 2, NT]) for s in range(2)]
        degm = [sbuf(f"degm{s}", [P, 2, NT]) for s in range(2)]
        rdeg = [sbuf(f"rdeg{s}", [P, 2, NT]) for s in range(2)]
        coef = [sbuf(f"coef{s}", [P, 2, NT]) for s in range(2)]
        psum = [ctx.enter_context(nc.psum_tensor(f"psum{s}", [P, 4, U], F32)) for s in range(2)]

        XH = [t[:, 0:2, :] for t in XS]
        XL = [t[:, 2:4, :] for t in XS]

        def cut(t, a, b, width):
            return t[:, a:b, :].rearrange("p a (c w) -> p (a c) w", w=width)

        HTH = [cut(t, 0, 2, nodes) for t in XS]
        HTL = [cut(t, 2, 4, nodes) for t in XS]
        YTH = [cut(t, 0, 2, nodes) for t in VS]
        YTL = [cut(t, 2, 4, nodes) for t in VS]
        VH = [t[:, 0:2, :] for t in VS]
        VL = [t[:, 2:4, :] for t in VS]
        ATT = [[f[:, u, :] for u in (6, 7, 2, 3)] for f in full]
        ATH = [t[:, 0:4, :] for t in ZS]
        ATL = [t[:, 4:8, :] for t in ZS]
        ZH = [[cut(t, 4 * k, 4 * k + 2, nodes) for k in range(2)] for t in ZS]
        ZL = [[cut(t, 4 * k + 2, 4 * k + 4, nodes) for k in range(2)] for t in ZS]
        KTH = [cut(t, 0, 1, nodes) for t in ZS]
        KTL = [cut(t, 1, 2, nodes) for t in ZS]

        def plain(ap):
            return ap.bitcast(F32)

        def halves(row):
            return row.rearrange("p (t m) -> p t m", m=nodes)

        def squares(row):
            return row.rearrange("p (t m) -> p t m", m=P)

        x_loaded = sems("x_loaded")
        xh_ready = sems("xh_ready")
        xl_ready = sems("xl_ready")
        yt_done = sems("yt_done")
        yth_ready = sems("yth_ready")
        ytl_ready = sems("ytl_ready")
        kmat_ready = sems("kmat_ready")
        kb_done = sems("kb_done")
        dq_ready = sems("dq_ready")
        rows_ready = sems("rows_ready")
        cols_exp = sems("cols_exp")
        rows_exp = sems("rows_exp")
        btmp_ready = sems("btmp_ready")
        att_ready = sems("att_ready")
        ath_ready = sems("ath_ready")
        atl_ready = sems("atl_ready")
        att_sum = sems("att_sum")
        s_done = sems("s_done")
        agg_done = sems("agg_done")
        smat_ready = sems("smat_ready")
        rb_done = sems("rb_done")
        rrow_ready = sems("rrow_ready")
        scaled_ready = sems("scaled_ready")
        relu_ready = sems("relu_ready")
        res_ready = sems("res_ready")
        stats_ready = sems("stats_ready")
        var_ready = sems("var_ready")
        rstd_ready = sems("rstd_ready")
        cur_ready = sems("cur_ready")
        ht_done = sems("ht_done")
        hth_ready = sems("hth_ready")
        htl_ready = sems("htl_ready")
        z_done = sems("z_done")
        zh_ready = sems("zh_ready")
        zl_ready = sems("zl_ready")
        gram_done = sems("gram_done")
        v_done = sems("v_done")
        vh_ready = sems("vh_ready")
        vl_ready = sems("vl_ready")
        sq_ready = sems("sq_ready")
        rn_ready = sems("rn_ready")
        mat_ready = sems("mat_ready")
        bc_done = sems("bc_done")
        sqrow_ready = sems("sqrow_ready")
        dist_ready = sems("dist_ready")
        gauss_ready = sems("gauss_ready")
        coef_ready = sems("coef_ready")
        ag_ready = sems("ag_ready")
        k_ready = sems("k_ready")
        kt_done = sems("kt_done")
        kth_ready = sems("kth_ready")
        ktl_ready = sems("ktl_ready")
        kv_done = sems("kv_done")
        x2h_ready = sems("x2h_ready")
        x2l_ready = sems("x2l_ready")
        l2_done = sems("l2_done")
        stored = sems("stored")
        dve_link = sems("dve_link")

        adj_loaded = sem("adj_loaded")
        small_loaded = sem("small_loaded")
        w_loaded = [sem(f"w_loaded{n}") for n in range(8)]
        zeros_ready = sem("zeros_ready")
        ident_ready = sem("ident_ready")
        prep_link = sem("prep_link")
        prep_pe = sem("prep_pe")
        prep_hi = sem("prep_hi")
        prep_out = sem("prep_out")
        gate_exp = sem("gate_exp")
        adj_t_done = sem("adj_t_done")
        adj_prep = sem("adj_prep")

        half = [full[0][:, 0:4, :], full[0][:, 4:8, :], full[1][:, 0:4, :], full[1][:, 4:8, :]]
        jobs = [("l", 0, half[0]), ("g", 0, half[1]), ("o", 0, half[3]), ("vo", 0, half[2]),
                ("l", 1, half[1]), ("g", 1, half[0]), ("o", 1, half[3]), ("vo", 1, half[2])]
        o_transposed = [half[0], half[1]]
        loads = [(w1l, half[0], 0), (w1g, half[1], 0), (w1v, half[2], 0), (w1o, half[3], 0),
                 (w3l, half[1], 2), (w3o, half[3], 3), (w3g, half[0], 4), (w3v, half[2], 4)]
        needs = [[0], [1], [3], [2], [4], [6], [5], [7]]
        adj_nat = half[3][:, 0, :].rearrange("p (t m) -> p t m", m=nodes)
        adj_rhs = full[1][:, 5:7, 0:nodes + 2]
        w2_full = half[3][:, 3, :].rearrange("p (t m) -> p t m", m=nodes)

        scratch = [half[3][:, 1 + t, U - P:U] for t in range(NT)]

        block = ctx.enter_context(nc.Block())

        @block.sync
        def _(sp):
            sp.dma_start(adj_nat, adj.rearrange("(t p) m -> p t m", p=P)).then_inc(adj_loaded, 16)
            for c in range(NT):
                sp.dma_start(adj_rhs[:, c, nodes:nodes + 1],
                             wq[c * P:(c + 1) * P].unsqueeze(1)).then_inc(adj_loaded, 16)
                sp.dma_start(adj_rhs[:, c, nodes + 1:nodes + 2],
                             wk[c * P:(c + 1) * P].unsqueeze(1)).then_inc(adj_loaded, 16)
            sp.dma_start(half[0], w1l.rearrange("(t p) d -> p t d", p=P)).then_inc(w_loaded[0], 16)
            for c in range(NT):
                sp.dma_start(bm_col[:, c:c + 1],
                             bm[c * P:(c + 1) * P].unsqueeze(1)).then_inc(small_loaded, 16)
            sp.dma_start(bias2_row[:], bias2.unsqueeze(0).to_broadcast([P, U])).then_inc(small_loaded, 16)
            for l, (g, sg) in enumerate(((gate1, sigma1), (gate3, sigma3))):
                sp.dma_start(gate_in[:, l, 0:1], g.unsqueeze(0).to_broadcast([P, 1])).then_inc(small_loaded, 16)
                sp.dma_start(gate_in[:, l, 1:2], sg.unsqueeze(0).to_broadcast([P, 1])).then_inc(small_loaded, 16)
            for n in range(1, 8):
                src, dst, read = loads[n]
                if n == 3:
                    sp.wait_ge(adj_prep, 1)
                if read:
                    sp.wait_ge(prep_pe, 4 * read)
                sp.dma_start(dst, src.rearrange("(t p) d -> p t d", p=P)).then_inc(w_loaded[n], 16)

            def load(s, j):
                sp.dma_start(X[s], x_tiles[:, bass.ds((j * 2 + s) * NT, NT), :]).then_inc(x_loaded[s], 16)

            def store(s, j):
                sp.wait_ge(cur_ready[s], j * 8 + 8)
                sp.dma_start(out_tiles[:, bass.ds((j * 2 + s) * NT, NT), :], CUR[s]).then_inc(stored[s], 16)

            sp.wait_ge(prep_pe, 32)
            load(0, 0)
            load(1, 0)
            with sp.Fori(0, TURNS - 1) as i:
                for s in range(2):
                    sp.wait_ge(res_ready[s], i * 8 + 2)
                    load(s, i + 1)
                store(0, i)
                store(1, i)
            for s in range(2):
                store(s, TURNS - 1)
            for s in range(2):
                sp.wait_ge(stored[s], 16 * TURNS)

        @block.tensor
        def _(pe):
            mm = nc.tensor.matmul

            def product(dst, terms, late=1, wait=None):
                early = [(a[0], a[2]) for a in terms] + [(a[1], a[2]) if late else (a[0], a[3]) for a in terms]
                last = [(a[0], a[3]) if late else (a[1], a[2]) for a in terms]
                for n, (a, b) in enumerate(early):
                    mm(dst, a, b, start=(n == 0), stop=False)
                if wait:
                    pe.wait_ge(*wait)
                for n, (a, b) in enumerate(last):
                    ins = mm(dst, a, b, start=False, stop=(n == len(last) - 1))
                return ins

            def flip(dst, src):
                return mm(dst, src, ident[:], is_transpose=True, start=True, stop=True)

            pe.wait_ge(ident_ready, 1)
            pe.wait_ge(adj_loaded, 16 * 5)
            for c in range(NT):
                for o in range(NT):
                    last = flip(psum[1][:, 3, c * nodes + o * P:c * nodes + (o + 1) * P],
                                adj_nat[:, o, c * P:(c + 1) * P])
            last.then_inc(adj_t_done, 1)
            for q, (kind, l, src) in enumerate(jobs):
                if q == 1:
                    pe.wait_ge(adj_prep, 1)
                for n in needs[q]:
                    pe.wait_ge(w_loaded[n], 16)
                if q >= 2:
                    pe.wait_ge(prep_out, 4 * (q - 1))
                if kind == "vo":
                    pe.wait_ge(prep_out, 4 * q)
                for t in range(FT):
                    dst = psum[q % 2][:, t, :]
                    for e in range(FT):
                        if kind == "vo":
                            last = mm(dst, src[:, e, t * P:(t + 1) * P], o_transposed[l][:, e, :],
                                      start=(e == 0), stop=(e == FT - 1))
                        else:
                            last = flip(dst[:, e * P:(e + 1) * P], src[:, e, t * P:(t + 1) * P])
                    last.then_inc(prep_pe, 1)

            def adj_x(s, j):
                pe.wait_ge(xh_ready[s], j + 1)
                pe.wait_ge(res_ready[s], j * 8)
                for t in range(FT):
                    cols = slice(t * P, (t + 1) * P)
                    product(psum[s][:, t, 0:nodes + 2],
                            [(XH[s][:, c, cols], XL[s][:, c, cols], adj_rhs_hi[:, c, :], adj_rhs_lo[:, c, :])
                             for c in range(NT)],
                            late=0, wait=(xl_ready[s], j + 1) if t == 0 else None).then_inc(yt_done[s], 1)

            def k_rows(s, j):
                pe.wait_ge(kmat_ready[s], j + 1)
                for t in range(FT):
                    flip(psum[s][:, 0, t * P:(t + 1) * P], squares(M[s][:, 2, :])[:, t, :])
                flip(psum[s][:, 1, 0:P], M[s][:, 3, 0:P]).then_inc(kb_done[s], 1)

            def aggregate(s, j):
                for t in range(FT):
                    pe.wait_ge(ath_ready[s], j * 4 + (t + 1))
                    for o, bank in enumerate((3, 0)):
                        for y in (YTH, YTL):
                            mm(psum[s][:, bank, :], y[s][:, t, o * P:(o + 1) * P], ATH[s][:, t, :],
                               start=(t == 0 and y is YTH), stop=False)
                    pe.wait_ge(atl_ready[s], j * 4 + (t + 1))
                    for o, bank in enumerate((3, 0)):
                        last = mm(psum[s][:, bank, :], YTH[s][:, t, o * P:(o + 1) * P], ATL[s][:, t, :],
                                  start=False, stop=(t == FT - 1))
                        if t == FT - 1:
                            last.then_inc(agg_done[s], 1)

            def softmax_sums(s, j):
                pe.wait_ge(att_sum[s], j * 3 + 3)
                for t in range(FT):
                    last = mm(psum[s][:, 2, t:t + 1], ATT[s][3][:, t * P:(t + 1) * P], ones[:],
                              start=True, stop=True)
                last.then_inc(s_done[s], 1)

            def sum_rows(s, j):
                pe.wait_ge(smat_ready[s], j + 1)
                for t in range(FT):
                    last = flip(psum[s][:, 1, t * P:(t + 1) * P], squares(M[s][:, 3, :])[:, t, :])
                last.then_inc(rb_done[s], 1)

            def transpose_x(s, j, l):
                for n in range(NT):
                    pe.wait_ge(cur_ready[s], j * 8 + (4 * l + n + 1))
                    for d in range(FT):
                        c = (d % 2) * nodes + n * P
                        last = flip(psum[s][:, 1 + d // 2, c:c + P], CUR[s][:, n, d * P:(d + 1) * P])
                        if n == NT - 1 and d % 2:
                            last.then_inc(ht_done[s], 1)

            def project(s, j, l, kind, e):
                if kind == 0 and e == 0:
                    pe.wait_ge(hth_ready[s], j * 4 + (2 * l + 2))
                bank = (3, 0, 1, 2)[2 * kind + e // 2]
                wh, wl = w_hi[l]["lg"[kind]], w_lo[l]["lg"[kind]]
                cols = slice(e * P, (e + 1) * P)
                last = product(psum[s][:, bank, (e % 2) * nodes:(e % 2 + 1) * nodes],
                               [(wh[:, d, cols], wl[:, d, cols], HTH[s][:, d, :], HTL[s][:, d, :])
                                for d in range(FT)],
                               wait=(htl_ready[s], j * 4 + (2 * l + 2)) if kind == 0 and e == 0 else None)
                if e % 2:
                    last.then_inc(z_done[s], 1)

            def gram(s, j, l, kind, n):
                if n == 0:
                    pe.wait_ge(zl_ready[s], j * 8 + (4 * l + 2 * kind + 1))
                    pe.wait_ge(zh_ready[s], j * 8 + (4 * l + 2 * kind + 2))
                zh, zl = ZH[s][kind], ZL[s][kind]
                cols = slice(n * P, (n + 1) * P)
                hi = [(zh[:, e, cols], zh[:, e, :]) for e in range(FT)]
                lo = [p for e in range(FT) for p in ((zh[:, e, cols], zl[:, e, :]), (zl[:, e, cols], zh[:, e, :]))]
                for i, (a, b) in enumerate(hi + lo):
                    if n == 0 and i == len(hi):
                        pe.wait_ge(zl_ready[s], j * 8 + (4 * l + 2 * kind + 2))
                    last = mm(psum[s][:, (3, 1)[kind], n * nodes:(n + 1) * nodes], a, b,
                              start=(i == 0), stop=(i == 3 * FT - 1))
                if n == NT - 1:
                    last.then_inc(gram_done[s], 1)

            def values(s, j, l, n):
                cols = slice(n * P, (n + 1) * P)
                wh, wl = w_hi[l]["vo"], w_lo[l]["vo"]
                product(psum[s][:, 2 * n, :],
                        [(HTH[s][:, d, cols], HTL[s][:, d, cols], wh[:, d, :], wl[:, d, :])
                         for d in range(FT)]).then_inc(v_done[s], 1)

            def norm_rows(s, j, l):
                pe.wait_ge(mat_ready[s], j * 2 + (l + 1))
                pe.wait_ge(vl_ready[s], j * 4 + (2 * l + 1))
                for t in range(4):
                    last = flip(psum[s][:, 0, t * P:(t + 1) * P], squares(M[s][:, 2, :])[:, t, :])
                last.then_inc(bc_done[s], 1)

            def transpose_k(s, j, l):
                pe.wait_ge(k_ready[s], j * 2 + (l + 1))
                for m in range(NT):
                    for n in range(NT):
                        last = flip(psum[s][:, 3, m * nodes + n * P:m * nodes + (n + 1) * P],
                                    halves(M[s][:, 0, :])[:, n, m * P:(m + 1) * P])
                last.then_inc(kt_done[s], 1)

            def mix_values(s, j, l):
                pe.wait_ge(kth_ready[s], j * 2 + (l + 1))
                pe.wait_ge(vl_ready[s], j * 4 + (2 * l + 2))
                for n in range(NT):
                    cols = slice(n * P, (n + 1) * P)
                    product(psum[s][:, n, :],
                            [(KTH[s][:, m, cols], KTL[s][:, m, cols], VH[s][:, m, :], VL[s][:, m, :])
                             for m in range(NT)],
                            late=0, wait=(ktl_ready[s], j * 2 + (l + 1)) if n == 0 else None).then_inc(kv_done[s], 1)

            def layer2(s, j):
                pe.wait_ge(x2h_ready[s], j * 2 + 2)
                for m in range(NT):
                    cols = slice(m * P, (m + 1) * P)
                    product(psum[s][:, 2 + m, :],
                            [(w2_hi[:, n, cols], w2_lo[:, n, cols], XH[s][:, n, :], XL[s][:, n, :])
                             for n in range(NT)],
                            wait=(x2l_ready[s], j * 2 + 2) if m == 0 else None).then_inc(l2_done[s], 1)

            def first_layer(s, j):
                adj_x(s, j)
                k_rows(s, j)
                aggregate(s, j)
                softmax_sums(s, j)
                sum_rows(s, j)
                transpose_x(s, j, 0)

            def middle_slot(s, js, l, r, jr):
                norm_rows(r, jr, 0)
                for e in range(FT):
                    project(s, js, l, 0, e)
                transpose_k(r, jr, 0)
                project(s, js, l, 1, 0)
                mix_values(r, jr, 0)
                for e in range(1, FT):
                    project(s, js, l, 1, e)
                gram(s, js, l, 0, 0)
                gram(s, js, l, 0, 1)
                layer2(r, jr)
                gram(s, js, l, 1, 0)
                gram(s, js, l, 1, 1)
                values(s, js, l, 0)
                transpose_x(r, jr, 1)
                values(s, js, l, 1)

            def seam_slot(s, js, l, r, jr, jn):
                if jr is not None:
                    norm_rows(r, jr, 1)
                for e in range(FT):
                    project(s, js, l, 0, e)
                if jr is not None:
                    transpose_k(r, jr, 1)
                project(s, js, l, 1, 0)
                if jr is not None:
                    mix_values(r, jr, 1)
                if jn is not None:
                    adj_x(r, jn)
                project(s, js, l, 1, 1)
                project(s, js, l, 1, 2)
                if jn is not None:
                    k_rows(r, jn)
                project(s, js, l, 1, 3)
                gram(s, js, l, 0, 0)
                gram(s, js, l, 0, 1)
                gram(s, js, l, 1, 0)
                if jn is not None:
                    aggregate(r, jn)
                    softmax_sums(r, jn)
                gram(s, js, l, 1, 1)
                if jn is not None:
                    sum_rows(r, jn)
                values(s, js, l, 0)
                values(s, js, l, 1)
                if jn is not None:
                    transpose_x(r, jn, 0)

            def tail(r, j):
                norm_rows(r, j, 1)
                transpose_k(r, j, 1)
                mix_values(r, j, 1)

            first_layer(0, 0)
            seam_slot(0, 0, 0, 1, None, 0)
            with pe.Fori(0, TURNS - 1) as i:
                middle_slot(1, i, 0, 0, i)
                middle_slot(0, i, 1, 1, i)
                seam_slot(1, i, 1, 0, i, i + 1)
                seam_slot(0, i + 1, 0, 1, i, i + 1)
            e = TURNS - 1
            middle_slot(1, e, 0, 0, e)
            middle_slot(0, e, 1, 1, e)
            seam_slot(1, e, 1, 0, e, None)
            tail(1, e)

        @block.scalar
        def _(act):
            def run(dst, src, func=ACT.Copy, **kw):
                return nc.scalar.activation(dst, src, func, **kw)

            act.wait_ge(small_loaded, 16 * 7)
            for l in range(2):
                run(gate_tmp[:, l, 0:1], gate_in[:, l, 0:1], ACT.Exp, scale=-1.0).then_inc(gate_exp, 1)
                run(inv_s2[l][:], gate_in[:, l, 1:2], ACT.Exp, scale=-2.0).then_inc(gate_exp, 1)
            for q, (kind, l, _) in enumerate(jobs):
                if kind == "o":
                    continue
                for t in range(FT):
                    act.wait_ge(prep_pe, 4 * q + t + 1)
                    run(w_hi[l][kind][:, t, :], psum[q % 2][:, t, :]).then_inc(prep_hi, 1)

            def split_x(s, j):
                act.wait_ge(x_loaded[s], j * 16 + 16)
                act.wait_ge(v_done[s], j * 4)
                run(XH[s], X[s]).then_inc(xh_ready[s], 1)

            def split_adj_x(s, j):
                act.wait_ge(kv_done[s], j * 4)
                for t in range(FT):
                    act.wait_ge(yt_done[s], j * 4 + (t + 1))
                    run(YTH[s][:, t, :], psum[s][:, t, 0:nodes]).then_inc(yth_ready[s], 1)

            def softmax_factors(s, j):
                act.wait_ge(dq_ready[s], j + 1)
                run(a_col[s][:], dq[s][:], ACT.Exp)
                run(b_col[s][:], dq[s][:], ACT.Exp, scale=SLOPE).then_inc(cols_exp[s], 1)
                act.wait_ge(rows_ready[s], j + 1)
                run(M[s][:, 1, :], M[s][:, 1, :], ACT.Exp, scale=SLOPE - 1.0)
                run(M[s][:, 0, :], M[s][:, 0, :], ACT.Exp, scale=1.0 - SLOPE).then_inc(rows_exp[s], 1)

            def low_slope(s, j, t):
                if t == 0:
                    act.wait_ge(cols_exp[s], j + 1)
                    act.wait_ge(rows_exp[s], j + 1)
                if t == 2:
                    act.wait_ge(stored[s], j * 16)
                run(ATT[s][t], M[s][:, 1, :], scale=b_col[s][:, t:t + 1]).then_inc(btmp_ready[s], 1)

            def split_att(s, j, t):
                act.wait_ge(att_ready[s], j * 4 + (t + 1))
                run(ATH[s][:, t, :], ATT[s][t]).then_inc(ath_ready[s], 1)

            def sum_row(s, j):
                act.wait_ge(rb_done[s], j + 1)
                run(M[s][:, 0, :], psum[s][:, 1, :]).then_inc(rrow_ready[s], 1)

            def relu_rows(s, j):
                for o in range(NT):
                    act.wait_ge(scaled_ready[s], j * 2 + (o + 1))
                    run(M[s][:, 1 + o, :], M[s][:, 1 + o, :], ACT.Relu,
                        bias=bm_col[:, o:o + 1]).then_inc(relu_ready[s], 1)

            def split_xt(s, j, l):
                for h in range(2):
                    act.wait_ge(ht_done[s], j * 4 + (2 * l + h + 1))
                    run(XH[s][:, h, :], psum[s][:, 1 + h, :]).then_inc(hth_ready[s], 1)

            def split_z(s, j, l, kind, part):
                act.wait_ge(z_done[s], j * 8 + (4 * l + 2 * kind + part + 1))
                run(ZS[s][:, 4 * kind + part, :],
                    psum[s][:, (3, 0, 1, 2)[2 * kind + part], :]).then_inc(zh_ready[s], 1)

            def split_v(s, j, l, n):
                act.wait_ge(v_done[s], j * 4 + (2 * l + n + 1))
                run(VH[s][:, n, :], psum[s][:, 2 * n, :]).then_inc(vh_ready[s], 1)

            def sq_row(s, j, l):
                act.wait_ge(bc_done[s], j * 2 + (l + 1))
                run(M[s][:, 3, 0:nodes], psum[s][:, 0, nodes:2 * nodes]).then_inc(sqrow_ready[s], 1)

            def gauss(s, j, l):
                act.wait_ge(dist_ready[s], j * 2 + (l + 1))
                m = halves(M[s][:, 1, :])
                for n in range(NT):
                    last = run(m[:, n, :], m[:, n, :], ACT.Exp, scale=inv_s2[l][:], bias=gbias[s][:, n:n + 1])
                last.then_inc(gauss_ready[s], 1)

            def weigh_gauss(s, j, l):
                act.wait_ge(coef_ready[s], j * 2 + (l + 1))
                m = halves(M[s][:, 1, :])
                for n in range(NT):
                    last = run(m[:, n, :], m[:, n, :], scale=coef[s][:, 1, n:n + 1])
                last.then_inc(ag_ready[s], 1)

            def split_kt(s, j, l):
                act.wait_ge(kt_done[s], j * 2 + (l + 1))
                run(ZS[s][:, 0, :], psum[s][:, 3, :]).then_inc(kth_ready[s], 1)

            def split_x2(s, j):
                for n in range(NT):
                    act.wait_ge(cur_ready[s], j * 8 + (2 + n + 1))
                    run(XH[s][:, n, :], CUR[s][:, n, :]).then_inc(x2h_ready[s], 1)

            def attention(s, j):
                low_slope(s, j, 0)
                low_slope(s, j, 1)
                split_att(s, j, 0)
                low_slope(s, j, 2)
                split_att(s, j, 1)
                low_slope(s, j, 3)
                split_att(s, j, 2)
                split_att(s, j, 3)

            def first_layer(s, j):
                split_x(s, j)
                split_adj_x(s, j)
                softmax_factors(s, j)
                attention(s, j)
                sum_row(s, j)
                relu_rows(s, j)
                split_xt(s, j, 0)

            def middle_slot(s, js, l, r, jr):
                sq_row(r, jr, 0)
                gauss(r, jr, 0)
                split_z(s, js, l, 0, 0)
                weigh_gauss(r, jr, 0)
                split_z(s, js, l, 0, 1)
                split_kt(r, jr, 0)
                split_z(s, js, l, 1, 0)
                split_x2(r, jr)
                split_z(s, js, l, 1, 1)
                split_v(s, js, l, 0)
                split_xt(r, jr, 1)
                split_v(s, js, l, 1)

            def seam_slot(s, js, l, r, jr, jn):
                if jr is not None:
                    sq_row(r, jr, 1)
                    gauss(r, jr, 1)
                split_z(s, js, l, 0, 0)
                if jr is not None:
                    weigh_gauss(r, jr, 1)
                if jn is not None:
                    split_x(r, jn)
                split_z(s, js, l, 0, 1)
                if jr is not None:
                    split_kt(r, jr, 1)
                if jn is not None:
                    split_adj_x(r, jn)
                split_z(s, js, l, 1, 0)
                if jn is not None:
                    softmax_factors(r, jn)
                split_z(s, js, l, 1, 1)
                if jn is not None:
                    attention(r, jn)
                    sum_row(r, jn)
                    relu_rows(r, jn)
                split_v(s, js, l, 0)
                split_v(s, js, l, 1)
                if jn is not None:
                    split_xt(r, jn, 0)

            def tail(r, j):
                sq_row(r, j, 1)
                gauss(r, j, 1)
                weigh_gauss(r, j, 1)
                split_kt(r, j, 1)

            first_layer(0, 0)
            seam_slot(0, 0, 0, 1, None, 0)
            with act.Fori(0, TURNS - 1) as i:
                middle_slot(1, i, 0, 0, i)
                middle_slot(0, i, 1, 1, i)
                seam_slot(1, i, 1, 0, i, i + 1)
                seam_slot(0, i + 1, 0, 1, i, i + 1)
            e = TURNS - 1
            middle_slot(1, e, 0, 0, e)
            middle_slot(0, e, 1, 1, e)
            seam_slot(1, e, 1, 0, e, None)
            tail(1, e)

        @block.vector
        def _(dve):
            tt = nc.vector.tensor_tensor
            ts = nc.vector.tensor_scalar
            stt = nc.vector.scalar_tensor_tensor

            links = [0, 0]

            def own(s, j, ins):
                links[s] += 1
                ins.then_inc(dve_link[s], 1)
                dve.wait_ge(dve_link[s], j * DVE_LINKS + links[s])

            def low(dst, src, hi):
                return tt(dst, src, plain(hi), ALU.subtract)

            prep = [0]

            def link(ins):
                prep[0] += 1
                ins.then_inc(prep_link, 1)
                dve.wait_ge(prep_link, prep[0])

            nc.vector.memset(minus_half[:], -0.5)
            nc.vector.memset(ones[:], 1.0)
            dve.wait_ge(adj_loaded, 16 * 5)
            dve.wait_ge(ident_ready, 1)
            dve.wait_ge(adj_t_done, 1)
            nc.vector.tensor_copy(adj_rhs[:, :, 0:nodes],
                                  psum[1][:, 3, :].rearrange("p (t m) -> p t m", m=nodes))
            nc.vector.tensor_copy(adj_off[:], adj_nat)
            link(tt(w2_full, adj_nat, adj_nat, ALU.mult))
            for t in range(NT):
                blk = slice(t * P, (t + 1) * P)
                tt(w2_full[:, t, blk], w2_full[:, t, blk], ident[:], ALU.add)
                link(tt(scratch[t], adj_nat[:, t, blk], ident[:], ALU.mult))
                link(tt(adj_off[:, t, blk], adj_nat[:, t, blk], scratch[t], ALU.subtract))
            nc.vector.tensor_copy(adj_rhs_hi[:], adj_rhs)
            link(nc.vector.tensor_copy(w2_hi[:], w2_full))
            low(adj_rhs_lo[:], adj_rhs, adj_rhs_hi[:])
            low(w2_lo[:], w2_full, w2_hi[:]).then_inc(adj_prep, 1)
            dve.wait_ge(gate_exp, 4)
            for l in range(2):
                link(ts(gate_tmp[:, l, 1:2], gate_tmp[:, l, 0:1], 1.0, None, ALU.add))
                link(nc.vector.reciprocal(mix[l][:, 0, 0:1], gate_tmp[:, l, 1:2]))
                nc.vector.tensor_copy(mix[l][:, 0, 1:2], mix[l][:, 0, 0:1])
                for n in range(NT):
                    link(ts(mix[l][:, 1, n:n + 1], mix[l][:, 0, 0:1], -1.0, 1.0, ALU.mult, ALU.add))
            hi = 0
            for q, (kind, l, _) in enumerate(jobs):
                for t in range(FT):
                    src = psum[q % 2][:, t, :]
                    if kind == "o":
                        dve.wait_ge(prep_pe, 4 * q + t + 1)
                        nc.vector.tensor_copy(o_transposed[l][:, t, :], src).then_inc(prep_out, 1)
                    else:
                        hi += 1
                        dve.wait_ge(prep_hi, hi)
                        low(w_lo[l][kind][:, t, :], src, w_hi[l][kind][:, t, :]).then_inc(prep_out, 1)

            def norm_stats(s, j, layer):
                for n in range(NT):
                    dve.wait_ge(res_ready[s], j * 8 + (2 * layer + n + 1))
                    ins = nc.vector.bn_stats(stats[s][:, n, :], CUR[s][:, n, :])
                ins.then_inc(stats_ready[s], 1)
                dve.wait_ge(stats_ready[s], j * 4 + (layer + 1))
                nc.vector.tensor_copy(count[s][:], stats[s][:, 0, 0:1])
                for n in range(NT):
                    ins = nc.vector.bn_aggr(mv[s][:, n, :], stats[s][:, n, :])
                own(s, j, ins)
                ts(veps[s][:], mv[s][:, :, 1], EPS_LN, None, ALU.add).then_inc(var_ready[s], 1)

            def normalise(s, j, layer):
                dve.wait_ge(rstd_ready[s], j * 4 + (layer + 1))
                for n in range(NT):
                    ins = ts(CUR[s][:, n, :], CUR[s][:, n, :], mv[s][:, n, 0:1], rstd[s][:, n:n + 1],
                             ALU.subtract, ALU.mult)
                    ins.then_inc(cur_ready[s], 1)

            def split_adj_x(s, j):
                for t in range(FT):
                    dve.wait_ge(yth_ready[s], j * 4 + (t + 1))
                    low(YTL[s][:, t, :], psum[s][:, t, 0:nodes], YTH[s][:, t, :]).then_inc(ytl_ready[s], 1)
                own(s, j, nc.vector.tensor_copy(qk[s][:], psum[s][:, :, nodes:nodes + 2]))
                own(s, j, nc.vector.reduce_max(qmax_col[s][:], qk[s][:, :, 0], AX.X))
                nc.vector.tensor_copy(squares(M[s][:, 2, :]), qk[s][:, :, 1:2].to_broadcast([P, FT, P]))
                nc.vector.tensor_copy(M[s][:, 3, 0:P],
                                      qmax_col[s][:].to_broadcast([P, P])).then_inc(kmat_ready[s], 1)

            def softmax_args(s, j):
                dve.wait_ge(kb_done[s], j + 1)
                own(s, j, nc.vector.reduce_max(qmax[s][:], psum[s][:, 1, 0:P], AX.X))
                ts(dq[s][:], qk[s][:, :, 0], qmax[s][:], None, ALU.subtract).then_inc(dq_ready[s], 1)
                ts(M[s][:, 1, :], psum[s][:, 0, :], qmax[s][:], 0.0, ALU.add, ALU.max)
                ts(M[s][:, 0, :], psum[s][:, 0, :], qmax[s][:], 0.0, ALU.add,
                   ALU.min).then_inc(rows_ready[s], 1)

            def attention(s, j):
                for t in range(FT):
                    dve.wait_ge(btmp_ready[s], j * 4 + (t + 1))
                    stt(ATT[s][t], M[s][:, 0, :], a_col[s][:, t:t + 1], ATT[s][t],
                        ALU.mult, ALU.max).then_inc(att_ready[s], 1)
                    if t:
                        split_att(s, j, t - 1)
                split_att(s, j, FT - 1)

            def split_att(s, j, t):
                dve.wait_ge(ath_ready[s], j * 4 + (t + 1))
                low(ATL[s][:, t, :], ATT[s][t], ATH[s][:, t, :]).then_inc(atl_ready[s], 1)

            def sum_squares(s, j):
                dve.wait_ge(s_done[s], j + 1)
                own(s, j, nc.vector.reciprocal(rsum[s][:], psum[s][:, 2, 0:FT]))
                nc.vector.tensor_copy(squares(M[s][:, 3, :]),
                                      rsum[s][:].unsqueeze(2).to_broadcast([P, FT, P])).then_inc(smat_ready[s], 1)

            def scale_agg(s, j):
                dve.wait_ge(rrow_ready[s], j + 1)
                for o, bank in enumerate((3, 0)):
                    dve.wait_ge(agg_done[s], j * 2 + (o + 1))
                    tt(M[s][:, 1 + o, :], psum[s][:, bank, :], M[s][:, 0, :],
                       ALU.mult).then_inc(scaled_ready[s], 1)

            def add_x(s, j):
                for o in range(NT):
                    dve.wait_ge(relu_ready[s], j * 2 + (o + 1))
                    ins = tt(CUR[s][:, o, :], M[s][:, 1 + o, :], X[s][:, o, :], ALU.add)
                    ins.then_inc(res_ready[s], 1)

            def split_xt(s, j, l):
                for h in range(2):
                    dve.wait_ge(hth_ready[s], j * 4 + (2 * l + h + 1))
                    low(XL[s][:, h, :], psum[s][:, 1 + h, :], XH[s][:, h, :]).then_inc(htl_ready[s], 1)

            def split_z(s, j, l, kind, part):
                dve.wait_ge(zh_ready[s], j * 8 + (4 * l + 2 * kind + part + 1))
                low(ZS[s][:, 4 * kind + 2 + part, :], psum[s][:, (3, 0, 1, 2)[2 * kind + part], :],
                    ZS[s][:, 4 * kind + part, :]).then_inc(zl_ready[s], 1)

            def split_v(s, j, l, n):
                dve.wait_ge(vh_ready[s], j * 4 + (2 * l + n + 1))
                low(VL[s][:, n, :], psum[s][:, 2 * n, :], VH[s][:, n, :]).then_inc(vl_ready[s], 1)

            def cosine_start(s, j, l):
                dve.wait_ge(gram_done[s], j * 4 + (2 * l + 1))
                for n in range(NT):
                    nc.vector.tensor_tensor_reduce(
                        squares(M[s][:, 2, :])[:, n, :], psum[s][:, 3, n * (nodes + P):n * (nodes + P) + P], ident[:],
                        1.0, 0.0, ALU.mult, ALU.add, diag[s][:, 0, n:n + 1])
                own(s, j, stt(halves(M[s][:, 0, :]), halves(psum[s][:, 3, :]), 0.0, adj_off[:],
                              ALU.max, ALU.mult))
                ts(sq_l[s][:], diag[s][:, 0, :], EPS_KERNEL ** 2, None, ALU.max)

            def gauss_start(s, j, l):
                dve.wait_ge(gram_done[s], j * 4 + (2 * l + 2))
                for n in range(NT):
                    ins = nc.vector.tensor_tensor_reduce(
                        squares(M[s][:, 2, :])[:, 2 + n, :], psum[s][:, 1, n * (nodes + P):n * (nodes + P) + P], ident[:],
                        1.0, 0.0, ALU.mult, ALU.add, diag[s][:, 1, n:n + 1])
                own(s, j, ins)
                own(s, j, ts(rnq[s][:, 1, :], diag[s][:, 1, :], -0.5, None, ALU.mult))
                ts(gbias[s][:], rnq[s][:, 1, :], inv_s2[l][:], None, ALU.mult).then_inc(sq_ready[s], 1)

            def norm_squares(s, j, l):
                dve.wait_ge(rn_ready[s], j * 2 + (l + 1))
                nc.vector.tensor_copy(
                    squares(M[s][:, 2, :]),
                    rnq[s][:].rearrange("p a b -> p (a b)").unsqueeze(2).to_broadcast([P, 4, P])
                ).then_inc(mat_ready[s], 1)

            def kernel_rows(s, j, l):
                dve.wait_ge(sqrow_ready[s], j * 2 + (l + 1))
                tt(halves(M[s][:, 1, :]), halves(psum[s][:, 1, :]),
                   M[s][:, 3:4, 0:nodes].to_broadcast([P, NT, nodes]), ALU.add).then_inc(dist_ready[s], 1)
                m = halves(M[s][:, 0, :])
                for n in range(NT):
                    ins = stt(m[:, n, :], psum[s][:, 0, 0:nodes], rnq[s][:, 0, n:n + 1], m[:, n, :],
                              ALU.mult, ALU.mult, accum_out=deg[s][:, 0, n:n + 1])
                own(s, j, ins)

            def kernel_weights(s, j, l):
                dve.wait_ge(gauss_ready[s], j * 2 + (l + 1))
                g = halves(M[s][:, 1, :])
                for n in range(NT):
                    ins = stt(g[:, n, :], g[:, n, :], 1.0, adj_off[:, n, :], ALU.min, ALU.mult,
                              accum_out=deg[s][:, 1, n:n + 1])
                own(s, j, ins)
                own(s, j, ts(degm[s][:], deg[s][:], EPS_KERNEL, None, ALU.max))
                own(s, j, nc.vector.reciprocal(rdeg[s][:], degm[s][:]))
                tt(coef[s][:], rdeg[s][:], mix[l][:], ALU.mult).then_inc(coef_ready[s], 1)

            def kernel_mix(s, j, l):
                dve.wait_ge(coef_ready[s], j * 2 + (l + 1))
                dve.wait_ge(ag_ready[s], j * 2 + (l + 1))
                m, g = halves(M[s][:, 0, :]), halves(M[s][:, 1, :])
                for n in range(NT):
                    ins = stt(m[:, n, :], m[:, n, :], coef[s][:, 0, n:n + 1], g[:, n, :], ALU.mult, ALU.add)
                ins.then_inc(k_ready[s], 1)

            def split_kt(s, j, l):
                dve.wait_ge(kth_ready[s], j * 2 + (l + 1))
                low(ZS[s][:, 1, :], psum[s][:, 3, :], ZS[s][:, 0, :]).then_inc(ktl_ready[s], 1)

            def add_kv(s, j, l):
                for n in range(NT):
                    dve.wait_ge(kv_done[s], j * 4 + (2 * l + n + 1))
                    tt(CUR[s][:, n, :], psum[s][:, n, :], CUR[s][:, n, :], ALU.add).then_inc(res_ready[s], 1)

            def split_x2(s, j):
                for n in range(NT):
                    dve.wait_ge(x2h_ready[s], j * 2 + (n + 1))
                    low(XL[s][:, n, :], CUR[s][:, n, :], XH[s][:, n, :]).then_inc(x2l_ready[s], 1)

            def add_bias2(s, j):
                for m in range(NT):
                    dve.wait_ge(l2_done[s], j * 2 + (m + 1))
                    tt(CUR[s][:, m, :], psum[s][:, 2 + m, :], bias2_row[:], ALU.add).then_inc(res_ready[s], 1)

            def first_layer(s, j):
                split_adj_x(s, j)
                softmax_args(s, j)
                attention(s, j)
                sum_squares(s, j)
                scale_agg(s, j)
                add_x(s, j)
                norm_stats(s, j, 0)
                normalise(s, j, 0)
                split_xt(s, j, 0)

            def middle_slot(s, js, l, r, jr):
                kernel_rows(r, jr, 0)
                kernel_weights(r, jr, 0)
                split_z(s, js, l, 0, 0)
                kernel_mix(r, jr, 0)
                split_z(s, js, l, 0, 1)
                split_kt(r, jr, 0)
                add_kv(r, jr, 0)
                norm_stats(r, jr, 1)
                split_z(s, js, l, 1, 0)
                normalise(r, jr, 1)
                split_x2(r, jr)
                split_z(s, js, l, 1, 1)
                cosine_start(s, js, l)
                add_bias2(r, jr)
                norm_stats(r, jr, 2)
                normalise(r, jr, 2)
                gauss_start(s, js, l)
                split_v(s, js, l, 0)
                norm_squares(s, js, l)
                split_xt(r, jr, 1)
                split_v(s, js, l, 1)

            def seam_slot(s, js, l, r, jr, jn):
                if jr is not None:
                    kernel_rows(r, jr, 1)
                    kernel_weights(r, jr, 1)
                split_z(s, js, l, 0, 0)
                if jr is not None:
                    kernel_mix(r, jr, 1)
                split_z(s, js, l, 0, 1)
                if jr is not None:
                    split_kt(r, jr, 1)
                    add_kv(r, jr, 1)
                    norm_stats(r, jr, 3)
                    end_batch(r, jr)
                if jn is not None:
                    split_adj_x(r, jn)
                if jr is not None:
                    normalise(r, jr, 3)
                split_z(s, js, l, 1, 0)
                if jn is not None:
                    softmax_args(r, jn)
                split_z(s, js, l, 1, 1)
                if jn is not None:
                    attention(r, jn)
                cosine_start(s, js, l)
                if jn is not None:
                    sum_squares(r, jn)
                    scale_agg(r, jn)
                    add_x(r, jn)
                    norm_stats(r, jn, 0)
                gauss_start(s, js, l)
                split_v(s, js, l, 0)
                if jn is not None:
                    normalise(r, jn, 0)
                norm_squares(s, js, l)
                split_v(s, js, l, 1)
                if jn is not None:
                    split_xt(r, jn, 0)

            def end_batch(s, j):
                assert links[s] in (0, DVE_LINKS), links
                links[s] = 0

            def tail(r, j):
                kernel_rows(r, j, 1)
                kernel_weights(r, j, 1)
                kernel_mix(r, j, 1)
                split_kt(r, j, 1)
                add_kv(r, j, 1)
                norm_stats(r, j, 3)
                normalise(r, j, 3)

            first_layer(0, 0)
            seam_slot(0, 0, 0, 1, None, 0)
            with dve.Fori(0, TURNS - 1) as i:
                middle_slot(1, i, 0, 0, i)
                middle_slot(0, i, 1, 1, i)
                seam_slot(1, i, 1, 0, i, i + 1)
                seam_slot(0, i + 1, 0, 1, i, i + 1)
            e = TURNS - 1
            middle_slot(1, e, 0, 0, e)
            middle_slot(0, e, 1, 1, e)
            seam_slot(1, e, 1, 0, e, None)
            tail(1, e)

        @block.gpsimd
        def _(pool):
            nc.gpsimd.memset(ident[:], 0.0).then_inc(zeros_ready, 1)
            pool.wait_ge(zeros_ready, 1)
            nc.gpsimd.affine_select(out=ident[:], in_=ident[:], compare_op=ALU.not_equal, fill=1.0, base=0,
                                    pattern=[[-1, P]], channel_multiplier=1).then_inc(ident_ready, 1)

            def split_x(s, j):
                pool.wait_ge(xh_ready[s], j + 1)
                nc.gpsimd.tensor_tensor(XL[s], X[s], plain(XH[s]), ALU.subtract).then_inc(xl_ready[s], 1)

            def add_att(s, j):
                for t in range(1, FT):
                    pool.wait_ge(atl_ready[s], j * 4 + (t + 1))
                    if t > 1:
                        pool.wait_ge(att_sum[s], j * 3 + (t - 1))
                    nc.gpsimd.tensor_tensor(ATT[s][t], ATT[s][t - 1], ATT[s][t], ALU.add).then_inc(att_sum[s], 1)

            def inverse_std(s, j, layer):
                pool.wait_ge(var_ready[s], j * 4 + (layer + 1))
                nc.gpsimd.tensor_tensor(rstd[s][:], veps[s][:], minus_half[:], ALU.pow).then_inc(rstd_ready[s], 1)

            def inverse_norm(s, j, l):
                pool.wait_ge(sq_ready[s], j * 2 + (l + 1))
                nc.gpsimd.tensor_tensor(rnq[s][:, 0, :], sq_l[s][:], minus_half[:],
                                        ALU.pow).then_inc(rn_ready[s], 1)

            def middle_slot(s, js, l, r, jr):
                inverse_std(r, jr, 1)
                inverse_std(r, jr, 2)
                inverse_norm(s, js, l)

            def seam_slot(s, js, l, r, jr, jn):
                if jn is not None:
                    split_x(r, jn)
                if jr is not None:
                    inverse_std(r, jr, 3)
                if jn is not None:
                    add_att(r, jn)
                    inverse_std(r, jn, 0)
                inverse_norm(s, js, l)

            split_x(0, 0)
            add_att(0, 0)
            inverse_std(0, 0, 0)
            seam_slot(0, 0, 0, 1, None, 0)
            with pool.Fori(0, TURNS - 1) as i:
                middle_slot(1, i, 0, 0, i)
                middle_slot(0, i, 1, 1, i)
                seam_slot(1, i, 1, 0, i, i + 1)
                seam_slot(0, i + 1, 0, 1, i, i + 1)
            e = TURNS - 1
            middle_slot(1, e, 0, 0, e)
            middle_slot(0, e, 1, 1, e)
            seam_slot(1, e, 1, 0, e, None)
            inverse_std(1, e, 3)


_INS = ["x", "adj", "L0_gnn_wq", "L0_gnn_wk", "L0_gnn_bm",
        "L1_gnn_W_lang", "L1_gnn_W_grav", "L1_gnn_W_V", "L1_gnn_W_O", "L1_gnn_gate_logit", "L1_gnn_log_sigma",
        "L2_gnn_bias",
        "L3_gnn_W_lang", "L3_gnn_W_grav", "L3_gnn_W_V", "L3_gnn_W_O", "L3_gnn_gate_logit", "L3_gnn_log_sigma"]
_OUTS = [((32, 256, 512), "float32")]


def kernel(**inputs):
    import numpy as _np
    import concourse.bacc as _bacc
    from concourse import mybir as _mybir
    from concourse.bass_utils import run_bass_kernel_spmd as _run

    nc = _bacc.Bacc("TRN2", target_bir_lowering=False, num_devices=1)
    arrays, args = {}, []
    for name in _INS:
        a = _np.ascontiguousarray(inputs[name])
        if a.ndim == 0:
            a = a.reshape(1)
        arrays[f"in_{name}_dram"] = a
        args.append(nc.dram_tensor(f"in_{name}_dram", a.shape, _mybir.dt.from_np(a.dtype), kind="ExternalInput").ap())
    for i, (shape, dtype) in enumerate(_OUTS):
        dt = _mybir.dt.from_np(_np.dtype(dtype))
        args.append(nc.dram_tensor(f"out_{i}_dram", shape, dt, kind="ExternalOutput").ap())
    gnn_stack(nc, *args)
    r = _run(nc, [arrays], core_ids=[0])
    return r.results[0]["out_0_dram"]
```

```python
from contextlib import ExitStack

import concourse.bass as bass
from concourse import mybir
from concourse.alu_op_type import AluOpType as ALU

F32 = mybir.dt.float32
F32R = mybir.dt.float32r
ACT = mybir.ActivationFunctionType
AX = mybir.AxisListType

P = 128
TILE_ORDER = (2, 1, 0, 3)
U = 512
EPS_LN = 1e-5
EPS_KERNEL = 1e-8
SLOPE = 0.01
DVE_LINKS = 18


def gnn_stack(nc, x, adj, wq, wk, bm, w1l, w1g, w1v, w1o, gate1, sigma1, bias2,
              w3l, w3g, w3v, w3o, gate3, sigma3, out):
    batches, nodes, feats = x.shape
    NT = nodes // P
    FT = feats // P
    TURNS = batches // 2
    x_tiles = x.rearrange("b (t p) n -> p (b t) n", p=P)
    out_tiles = out.rearrange("b (t p) n -> p (b t) n", p=P)

    ctx = ExitStack()
    with ctx:
        def sbuf(name, shape, dtype=F32):
            return ctx.enter_context(nc.sbuf_tensor(name, shape, dtype))

        def sem(name):
            return ctx.enter_context(nc.semaphore(name))

        def sems(name):
            return [sem(f"{name}{s}") for s in range(2)]

        ident = sbuf("ident", [P, P])
        ones = sbuf("ones", [P, 1])
        adj_rhs_hi = sbuf("adj_rhs_hi", [P, NT, nodes + 2], F32R)
        adj_rhs_lo = sbuf("adj_rhs_lo", [P, NT, nodes + 2], F32R)
        adj_off = sbuf("adj_off", [P, NT, nodes])
        w2_hi = sbuf("w2_hi", [P, NT, nodes], F32R)
        w2_lo = sbuf("w2_lo", [P, NT, nodes], F32R)
        bm_col = sbuf("bm_col", [P, NT])
        bias2_row = sbuf("bias2_row", [P, U])
        minus_half = sbuf("minus_half", [P, NT])
        gate_in = sbuf("gate_in", [P, 2, 2])
        gate_tmp = sbuf("gate_tmp", [P, 2, 2])
        mix = [sbuf(f"mix{l}", [P, 2]) for l in range(2)]
        inv_s2 = [sbuf(f"inv_s2{l}", [P, 1]) for l in range(2)]
        names = ("l", "g", "vo")
        w_hi = [{k: sbuf(f"w{l}{k}_hi", [P, FT, U], F32R) for k in names} for l in range(2)]
        w_lo = [{k: sbuf(f"w{l}{k}_lo", [P, FT, U], F32R) for k in names} for l in range(2)]

        full = [sbuf(f"full{s}", [P, 8, U]) for s in range(2)]
        X = [f[:, 0:2, :] for f in full]
        CUR = [f[:, 2:4, :] for f in full]
        M = [f[:, 4:8, :] for f in full]
        XS = [sbuf(f"xs{s}", [P, 4, U], F32R) for s in range(2)]
        ZS = [sbuf(f"zs{s}", [P, 8, U], F32R) for s in range(2)]
        VS = [sbuf(f"vs{s}", [P, 4, U], F32R) for s in range(2)]
        qk = [sbuf(f"qk{s}", [P, FT, 2]) for s in range(2)]
        qmax_col = [sbuf(f"qmax_col{s}", [P, 1]) for s in range(2)]
        qmax = [sbuf(f"qmax{s}", [P, 1]) for s in range(2)]
        dq = [sbuf(f"dq{s}", [P, FT]) for s in range(2)]
        a_col = [sbuf(f"a_col{s}", [P, FT]) for s in range(2)]
        b_col = [sbuf(f"b_col{s}", [P, FT]) for s in range(2)]
        rsum = [sbuf(f"rsum{s}", [P, FT]) for s in range(2)]
        stats = [sbuf(f"stats{s}", [P, NT, 6]) for s in range(2)]
        mv = [sbuf(f"mv{s}", [P, NT, 2]) for s in range(2)]
        count = [sbuf(f"count{s}", [P, 1]) for s in range(2)]
        veps = [sbuf(f"veps{s}", [P, NT]) for s in range(2)]
        rstd = [sbuf(f"rstd{s}", [P, NT]) for s in range(2)]
        diag = [sbuf(f"diag{s}", [P, 2, NT]) for s in range(2)]
        sq_l = [sbuf(f"sq_l{s}", [P, NT]) for s in range(2)]
        rnq = [sbuf(f"rnq{s}", [P, 2, NT]) for s in range(2)]
        gbias = [sbuf(f"gbias{s}", [P, NT]) for s in range(2)]
        deg = [sbuf(f"deg{s}", [P, 2, NT]) for s in range(2)]
        degm = [sbuf(f"degm{s}", [P, 2, NT]) for s in range(2)]
        rdeg = [sbuf(f"rdeg{s}", [P, 2, NT]) for s in range(2)]
        coef = [sbuf(f"coef{s}", [P, NT]) for s in range(2)]
        psum = [ctx.enter_context(nc.psum_tensor(f"psum{s}", [P, 4, U], F32)) for s in range(2)]

        XH = [t[:, 0:2, :] for t in XS]
        XL = [t[:, 2:4, :] for t in XS]

        def cut(t, a, b, width):
            return t[:, a:b, :].rearrange("p a (c w) -> p (a c) w", w=width)

        HTH = [cut(t, 0, 2, nodes) for t in XS]
        HTL = [cut(t, 2, 4, nodes) for t in XS]
        YTH = [cut(t, 2, 4, nodes) for t in ZS]
        YTL = [cut(t, 4, 6, nodes) for t in ZS]
        VH = [t[:, 0:2, :] for t in VS]
        VL = [t[:, 2:4, :] for t in VS]
        ATT = [[f[:, u, :] for u in (6, 7, 7, 5)] for f in full]
        ATH = [[t[:, u, :] for u in range(4)] for t in VS]
        ATL = [[t[:, u, :] for u in (0, 1, 6, 7)] for t in ZS]
        ZH = [[cut(t, 4 * k, 4 * k + 2, nodes) for k in range(2)] for t in ZS]
        ZL = [[cut(t, 4 * k + 2, 4 * k + 4, nodes) for k in range(2)] for t in ZS]
        KTH = [cut(t, 0, 1, nodes) for t in ZS]
        KTL = [cut(t, 1, 2, nodes) for t in ZS]

        def plain(ap):
            return ap.bitcast(F32)

        def halves(row):
            return row.rearrange("p (t m) -> p t m", m=nodes)

        def squares(row):
            return row.rearrange("p (t m) -> p t m", m=P)

        x_loaded = sems("x_loaded")
        xh_ready = sems("xh_ready")
        xl_ready = sems("xl_ready")
        yt_done = sems("yt_done")
        yth_ready = sems("yth_ready")
        ytl_ready = sems("ytl_ready")
        kmat_ready = sems("kmat_ready")
        kb_done = sems("kb_done")
        dq_ready = sems("dq_ready")
        rows_ready = sems("rows_ready")
        cols_exp = sems("cols_exp")
        rows_exp = sems("rows_exp")
        btmp_ready = sems("btmp_ready")
        att_ready = sems("att_ready")
        ath_ready = sems("ath_ready")
        atl_ready = sems("atl_ready")
        att_sum = sems("att_sum")
        s_done = sems("s_done")
        agg_done = sems("agg_done")
        smat_ready = sems("smat_ready")
        rb_done = sems("rb_done")
        rrow_ready = sems("rrow_ready")
        scaled_ready = sems("scaled_ready")
        relu_ready = sems("relu_ready")
        res_ready = sems("res_ready")
        stats_ready = sems("stats_ready")
        mean_ready = sems("mean_ready")
        var_ready = sems("var_ready")
        rstd_ready = sems("rstd_ready")
        cur_ready = sems("cur_ready")
        ht_done = sems("ht_done")
        hth_ready = sems("hth_ready")
        htl_ready = sems("htl_ready")
        z_done = sems("z_done")
        zh_ready = sems("zh_ready")
        zl_ready = sems("zl_ready")
        gram_done = sems("gram_done")
        v_done = sems("v_done")
        vh_ready = sems("vh_ready")
        vl_ready = sems("vl_ready")
        sq_ready = sems("sq_ready")
        rn_ready = sems("rn_ready")
        mat_ready = sems("mat_ready")
        bc_done = sems("bc_done")
        masked_ready = sems("masked_ready")
        sqrow_ready = sems("sqrow_ready")
        dist_ready = sems("dist_ready")
        cos_ready = sems("cos_ready")
        gauss_ready = sems("gauss_ready")
        k_ready = sems("k_ready")
        kt_done = sems("kt_done")
        kth_ready = sems("kth_ready")
        ktl_ready = sems("ktl_ready")
        kv_done = sems("kv_done")
        x2h_ready = sems("x2h_ready")
        x2l_ready = sems("x2l_ready")
        l2_done = sems("l2_done")
        stored = sems("stored")
        dve_link = sems("dve_link")

        adj_loaded = sem("adj_loaded")
        small_loaded = sem("small_loaded")
        w_loaded = [sem(f"w_loaded{n}") for n in range(8)]
        zeros_ready = sem("zeros_ready")
        ident_ready = sem("ident_ready")
        prep_link = sem("prep_link")
        prep_pe = sem("prep_pe")
        prep_hi = sem("prep_hi")
        prep_out = sem("prep_out")
        wv_rounded = sem("wv_rounded")
        wv_split = sem("wv_split")
        gate_exp = sem("gate_exp")
        adj_t_done = sem("adj_t_done")
        adj_prep = sem("adj_prep")

        jobs = [("l", 0), ("o", 0), ("vo", 0), ("g", 0), ("l", 1), ("o", 1), ("vo", 1), ("g", 1)]
        nat_a, nat_b = full[1][:, 0:4, :], full[1][:, 4:8, :]
        nat = {"l": nat_a, "o": nat_a, "g": nat_b}
        loads = [(w1l, nat_a, None, 0), (w1v, nat_b, None, 0), (w1o, nat_a, prep_pe, 4), (w1g, nat_b, wv_split, 2),
                 (w3l, nat_a, prep_pe, 8), (w3v, nat_b, prep_pe, 16), (w3o, nat_a, prep_pe, 20),
                 (w3g, nat_b, wv_split, 4)]
        load_of_job = {0: 0, 1: 2, 3: 3, 4: 4, 5: 6, 7: 7}
        load_of_wv = (1, 5)
        wv_hi, wv_lo = XS[1], VS[1]
        hi_of = {(k, l): w_hi[l][k] for l in range(2) for k in names}
        lo_of = {(k, l): w_lo[l][k] for l in range(2) for k in names}
        for l in range(2):
            hi_of["o", l], lo_of["o", l] = ZS[1][:, 0:4, :], ZS[1][:, 4:8, :]
        adj_nat = full[0][:, 2, :].rearrange("p (t m) -> p t m", m=nodes)
        adj_rhs = full[0][:, 3:5, 0:nodes + 2]
        scratch = [full[0][:, 3 + t, U - P:U] for t in range(NT)]
        w2_full = full[0][:, 5, :].rearrange("p (t m) -> p t m", m=nodes)

        block = ctx.enter_context(nc.Block())

        @block.sync
        def _(sp):
            sp.dma_start(adj_nat, adj.rearrange("(t p) m -> p t m", p=P)).then_inc(adj_loaded, 16)
            for c in range(NT):
                sp.dma_start(adj_rhs[:, c, nodes:nodes + 1],
                             wq[c * P:(c + 1) * P].unsqueeze(1)).then_inc(adj_loaded, 16)
                sp.dma_start(adj_rhs[:, c, nodes + 1:nodes + 2],
                             wk[c * P:(c + 1) * P].unsqueeze(1)).then_inc(adj_loaded, 16)
            for n in range(2):
                src, dst, _, _ = loads[n]
                sp.dma_start(dst, src.rearrange("(t p) d -> p t d", p=P)).then_inc(w_loaded[n], 16)
                if n == 0:
                    sp.dma_start(X[0], x_tiles[:, 0:NT, :]).then_inc(x_loaded[0], 16)
            for c in range(NT):
                sp.dma_start(bm_col[:, c:c + 1],
                             bm[c * P:(c + 1) * P].unsqueeze(1)).then_inc(small_loaded, 16)
            sp.dma_start(bias2_row[:], bias2.unsqueeze(0).to_broadcast([P, U])).then_inc(small_loaded, 16)
            for l, (g, sg) in enumerate(((gate1, sigma1), (gate3, sigma3))):
                sp.dma_start(gate_in[:, l, 0:1], g.unsqueeze(0).to_broadcast([P, 1])).then_inc(small_loaded, 16)
                sp.dma_start(gate_in[:, l, 1:2], sg.unsqueeze(0).to_broadcast([P, 1])).then_inc(small_loaded, 16)
            for n in range(2, 8):
                src, dst, read, reads = loads[n]
                sp.wait_ge(read, reads)
                sp.dma_start(dst, src.rearrange("(t p) d -> p t d", p=P)).then_inc(w_loaded[n], 16)

            def load(s, j):
                sp.dma_start(X[s], x_tiles[:, bass.ds((j * 2 + s) * NT, NT), :]).then_inc(x_loaded[s], 16)

            def store(s, j):
                sp.wait_ge(cur_ready[s], j * 8 + 8)
                sp.dma_start(out_tiles[:, bass.ds((j * 2 + s) * NT, NT), :], CUR[s]).then_inc(stored[s], 16)

            sp.wait_ge(prep_pe, 24)
            load(1, 0)
            with sp.Fori(0, TURNS - 1) as i:
                for s in range(2):
                    sp.wait_ge(res_ready[s], i * 8 + 2)
                    load(s, i + 1)
                store(0, i)
                store(1, i)
            for s in range(2):
                store(s, TURNS - 1)
            for s in range(2):
                sp.wait_ge(stored[s], 16 * TURNS)

        @block.tensor
        def _(pe):
            mm = nc.tensor.matmul

            def product(dst, terms, late=1, wait=None):
                early = [(a[0], a[2]) for a in terms] + [(a[1], a[2]) if late else (a[0], a[3]) for a in terms]
                last = [(a[0], a[3]) if late else (a[1], a[2]) for a in terms]
                for n, (a, b) in enumerate(early):
                    mm(dst, a, b, start=(n == 0), stop=False)
                if wait:
                    pe.wait_ge(*wait)
                for n, (a, b) in enumerate(last):
                    ins = mm(dst, a, b, start=False, stop=(n == len(last) - 1))
                return ins

            def flip(dst, src):
                return mm(dst, src, ident[:], is_transpose=True, start=True, stop=True)

            pe.wait_ge(ident_ready, 1)
            pe.wait_ge(adj_loaded, 16 * 5)
            for c in range(NT):
                for o in range(NT):
                    last = flip(psum[1][:, 3, c * nodes + o * P:c * nodes + (o + 1) * P],
                                adj_nat[:, o, c * P:(c + 1) * P])
            last.then_inc(adj_t_done, 1)

            def prepare(q):
                kind, l = jobs[q]
                if kind == "vo":
                    pe.wait_ge(prep_out, 4 * q)
                    pe.wait_ge(wv_split, 2 * l + 2)
                else:
                    pe.wait_ge(w_loaded[load_of_job[q]], 16)
                for t in range(FT):
                    dst = psum[1][:, t, :]
                    if q:
                        pe.wait_ge(prep_out, 4 * (q - 1) + t + 1)
                    elif t == 3:
                        pe.wait_ge(adj_prep, 1)
                    cols = slice(t * P, (t + 1) * P)
                    if kind == "vo":
                        last = product(dst, [(wv_hi[:, e, cols], wv_lo[:, e, cols],
                                              hi_of["o", l][:, e, :], lo_of["o", l][:, e, :]) for e in range(FT)])
                    else:
                        for e in range(FT):
                            last = flip(dst[:, e * P:(e + 1) * P], nat[kind][:, e, cols])
                    last.then_inc(prep_pe, 1)

            def adj_x(s, j):
                pe.wait_ge(xh_ready[s], j + 1)
                pe.wait_ge(cos_ready[s], j * 2)
                for t in TILE_ORDER:
                    cols = slice(t * P, (t + 1) * P)
                    product(psum[s][:, t, 0:nodes + 2],
                            [(XH[s][:, c, cols], XL[s][:, c, cols], adj_rhs_hi[:, c, :], adj_rhs_lo[:, c, :])
                             for c in range(NT)],
                            late=0, wait=(xl_ready[s], j + 1) if t == TILE_ORDER[0] else None).then_inc(yt_done[s], 1)

            def k_rows(s, j):
                pe.wait_ge(kmat_ready[s], j + 1)
                for t in range(FT):
                    flip(psum[s][:, 2, t * P:(t + 1) * P], squares(M[s][:, 2, :])[:, t, :])
                flip(psum[s][:, 1, 0:P], M[s][:, 3, 0:P]).then_inc(kb_done[s], 1)

            def aggregate(s, j, tiles, jp=None):
                if jp is not None:
                    pe.wait_ge(res_ready[s], jp * 8 + 7)
                for t in tiles:
                    pe.wait_ge(ath_ready[s], j * 4 + (t + 1))
                    for o, bank in enumerate((3, 0)):
                        for y in (YTH, YTL):
                            mm(psum[s][:, bank, :], y[s][:, t, o * P:(o + 1) * P], ATH[s][t],
                               start=(t == 0 and y is YTH), stop=False)
                    pe.wait_ge(atl_ready[s], j * 4 + (t + 1))
                    for o, bank in enumerate((3, 0)):
                        last = mm(psum[s][:, bank, :], YTH[s][:, t, o * P:(o + 1) * P], ATL[s][t],
                                  start=False, stop=(t == FT - 1))
                        if t == FT - 1:
                            last.then_inc(agg_done[s], 1)

            def softmax_sums(s, j):
                pe.wait_ge(att_sum[s], j * 3 + 3)
                for t in range(FT):
                    last = mm(psum[s][:, 2, t:t + 1], ATT[s][0][:, t * P:(t + 1) * P], ones[:],
                              start=True, stop=True)
                last.then_inc(s_done[s], 1)

            def sum_rows(s, j):
                pe.wait_ge(smat_ready[s], j + 1)
                for t in range(FT):
                    last = flip(psum[s][:, 1, t * P:(t + 1) * P], squares(M[s][:, 3, :])[:, t, :])
                last.then_inc(rb_done[s], 1)

            def transpose_x(s, j, l):
                for h in range(2):
                    for n in range(NT):
                        if h == 0:
                            pe.wait_ge(cur_ready[s], j * 8 + (4 * l + n + 1))
                        for d in range(2):
                            c = (2 * h + d) * P
                            last = flip(psum[s][:, 1 + h, d * nodes + n * P:d * nodes + (n + 1) * P],
                                        CUR[s][:, n, c:c + P])
                    last.then_inc(ht_done[s], 1)

            def project(s, j, l, kind, e):
                bank = (3, 0, 1, 2)[2 * kind + e // 2]
                dst = psum[s][:, bank, (e % 2) * nodes:(e % 2 + 1) * nodes]
                wh, wl = w_hi[l]["lg"[kind]], w_lo[l]["lg"[kind]]
                cols = slice(e * P, (e + 1) * P)
                first = kind == 0 and e == 0
                for h in range(2):
                    if first:
                        pe.wait_ge(hth_ready[s], j * 4 + (2 * l + h + 1))
                    for d in (2 * h, 2 * h + 1):
                        mm(dst, wh[:, d, cols], HTH[s][:, d, :], start=(d == 0), stop=False)
                        mm(dst, wl[:, d, cols], HTH[s][:, d, :], start=False, stop=False)
                for h in range(2):
                    if first:
                        pe.wait_ge(htl_ready[s], j * 4 + (2 * l + h + 1))
                    for d in (2 * h, 2 * h + 1):
                        last = mm(dst, wh[:, d, cols], HTL[s][:, d, :], start=False, stop=(d == FT - 1))
                if e % 2:
                    last.then_inc(z_done[s], 1)

            def gram(s, j, l, kind, n):
                if n == 0:
                    pe.wait_ge(zl_ready[s], j * 8 + (4 * l + 2 * kind + 1))
                    pe.wait_ge(zh_ready[s], j * 8 + (4 * l + 2 * kind + 2))
                zh, zl = ZH[s][kind], ZL[s][kind]
                cols = slice(n * P, (n + 1) * P)
                hi = [(zh[:, e, cols], zh[:, e, :]) for e in range(FT)]
                lo = [p for e in range(FT) for p in ((zh[:, e, cols], zl[:, e, :]), (zl[:, e, cols], zh[:, e, :]))]
                for i, (a, b) in enumerate(hi + lo):
                    if n == 0 and i == len(hi):
                        pe.wait_ge(zl_ready[s], j * 8 + (4 * l + 2 * kind + 2))
                    last = mm(psum[s][:, (3, 1)[kind], n * nodes:(n + 1) * nodes], a, b,
                              start=(i == 0), stop=(i == 3 * FT - 1))
                if n == NT - 1:
                    last.then_inc(gram_done[s], 1)

            def values(s, j, l, n):
                cols = slice(n * P, (n + 1) * P)
                wh, wl = w_hi[l]["vo"], w_lo[l]["vo"]
                product(psum[s][:, 2 * n, :],
                        [(HTH[s][:, d, cols], HTL[s][:, d, cols], wh[:, d, :], wl[:, d, :])
                         for d in range(FT)]).then_inc(v_done[s], 1)

            def norm_rows(s, j, l):
                pe.wait_ge(mat_ready[s], j * 2 + (l + 1))
                pe.wait_ge(vl_ready[s], j * 4 + (2 * l + 1))
                for t in range(4):
                    last = flip(psum[s][:, 0, t * P:(t + 1) * P], squares(M[s][:, 2, :])[:, t, :])
                last.then_inc(bc_done[s], 1)

            def transpose_k(s, j, l, lo_next=None):
                pe.wait_ge(k_ready[s], j * 2 + (l + 1))
                if l == 1 and lo_next is not None:
                    pe.wait_ge(ytl_ready[s], lo_next * 4 + 4)
                for m in range(NT):
                    for n in range(NT):
                        last = flip(psum[s][:, 3, m * nodes + n * P:m * nodes + (n + 1) * P],
                                    halves(M[s][:, 0, :])[:, n, m * P:(m + 1) * P])
                last.then_inc(kt_done[s], 1)

            def mix_values(s, j, l, lo_next=None):
                pe.wait_ge(kth_ready[s], j * 2 + (l + 1))
                pe.wait_ge(vl_ready[s], j * 4 + (2 * l + 2))
                for n in range(NT):
                    if n == 1 and lo_next is not None:
                        pe.wait_ge(dq_ready[s], lo_next + 1)
                    cols = slice(n * P, (n + 1) * P)
                    product(psum[s][:, n, :],
                            [(KTH[s][:, m, cols], KTL[s][:, m, cols], VH[s][:, m, :], VL[s][:, m, :])
                             for m in range(NT)],
                            late=0, wait=(ktl_ready[s], j * 2 + (l + 1)) if n == 0 else None).then_inc(kv_done[s], 1)

            def layer2(s, j):
                pe.wait_ge(x2h_ready[s], j * 2 + 2)
                for m in range(NT):
                    cols = slice(m * P, (m + 1) * P)
                    product(psum[s][:, 2 + m, :],
                            [(w2_hi[:, n, cols], w2_lo[:, n, cols], XH[s][:, n, :], XL[s][:, n, :])
                             for n in range(NT)],
                            wait=(x2l_ready[s], j * 2 + 2) if m == 0 else None).then_inc(l2_done[s], 1)

            def start():
                prepare(0)
                pe.wait_ge(adj_prep, 1)
                adj_x(0, 0)
                prepare(1)
                k_rows(0, 0)
                prepare(2)
                prepare(3)
                prepare(4)
                aggregate(0, 0, (0, 1, 2, 3))
                prepare(5)
                softmax_sums(0, 0)
                sum_rows(0, 0)
                prepare(6)
                prepare(7)
                transpose_x(0, 0, 0)

            def middle_slot(s, js, l, r, jr):
                norm_rows(r, jr, 0)
                for e in range(FT):
                    project(s, js, l, 0, e)
                transpose_k(r, jr, 0)
                project(s, js, l, 1, 0)
                mix_values(r, jr, 0)
                for e in range(1, FT):
                    project(s, js, l, 1, e)
                gram(s, js, l, 0, 0)
                gram(s, js, l, 0, 1)
                layer2(r, jr)
                gram(s, js, l, 1, 0)
                gram(s, js, l, 1, 1)
                values(s, js, l, 0)
                transpose_x(r, jr, 1)
                values(s, js, l, 1)

            def seam_slot(s, js, l, r, jr, jn):
                if jr is not None:
                    norm_rows(r, jr, 1)
                for e in range(3):
                    project(s, js, l, 0, e)
                if jr is None:
                    pe.wait_ge(prep_out, 4 * len(jobs))
                if jn is not None:
                    adj_x(r, jn)
                project(s, js, l, 0, 3)
                project(s, js, l, 1, 0)
                if jn is not None:
                    k_rows(r, jn)
                if jr is not None:
                    transpose_k(r, jr, 1, jn)
                project(s, js, l, 1, 1)
                if jr is not None:
                    mix_values(r, jr, 1, jn)
                project(s, js, l, 1, 2)
                project(s, js, l, 1, 3)
                if jn is not None:
                    aggregate(r, jn, (0, 1), jr)
                gram(s, js, l, 0, 0)
                if jn is not None:
                    aggregate(r, jn, (2, 3))
                    softmax_sums(r, jn)
                gram(s, js, l, 0, 1)
                if jn is not None:
                    sum_rows(r, jn)
                gram(s, js, l, 1, 0)
                gram(s, js, l, 1, 1)
                values(s, js, l, 0)
                values(s, js, l, 1)
                if jn is not None:
                    transpose_x(r, jn, 0)

            def tail(r, j):
                norm_rows(r, j, 1)
                transpose_k(r, j, 1)
                mix_values(r, j, 1)

            start()
            seam_slot(0, 0, 0, 1, None, 0)
            with pe.Fori(0, TURNS - 1) as i:
                middle_slot(1, i, 0, 0, i)
                middle_slot(0, i, 1, 1, i)
                seam_slot(1, i, 1, 0, i, i + 1)
                seam_slot(0, i + 1, 0, 1, i, i + 1)
            e = TURNS - 1
            middle_slot(1, e, 0, 0, e)
            middle_slot(0, e, 1, 1, e)
            seam_slot(1, e, 1, 0, e, None)
            tail(1, e)

        @block.scalar
        def _(act):
            def run(dst, src, func=ACT.Copy, **kw):
                return nc.scalar.activation(dst, src, func, **kw)

            def prepare(q, tiles=range(FT)):
                for t in tiles:
                    act.wait_ge(prep_pe, 4 * q + t + 1)
                    run(hi_of[jobs[q]][:, t, :], psum[1][:, t, :]).then_inc(prep_hi, 1)

            def round_wv(l):
                act.wait_ge(w_loaded[load_of_wv[l]], 16)
                for h in range(2):
                    run(wv_hi[:, 2 * h:2 * h + 2, :], nat_b[:, 2 * h:2 * h + 2, :]).then_inc(wv_rounded, 1)

            def gates():
                act.wait_ge(small_loaded, 16 * 7)
                for l in range(2):
                    run(gate_tmp[:, l, 0:1], gate_in[:, l, 0:1], ACT.Exp, scale=-1.0).then_inc(gate_exp, 1)
                    run(inv_s2[l][:], gate_in[:, l, 1:2], ACT.Exp, scale=-2.0).then_inc(gate_exp, 1)

            def split_x(s, j):
                act.wait_ge(x_loaded[s], j * 16 + 16)
                act.wait_ge(v_done[s], j * 4)
                run(XH[s], X[s]).then_inc(xh_ready[s], 1)

            def split_adj_x(s, j):
                for n, t in enumerate(TILE_ORDER):
                    act.wait_ge(yt_done[s], j * 4 + (n + 1))
                    run(YTH[s][:, t, :], psum[s][:, t, 0:nodes]).then_inc(yth_ready[s], 1)

            def softmax_columns(s, j):
                act.wait_ge(dq_ready[s], j + 1)
                run(a_col[s][:], dq[s][:], ACT.Exp)
                run(b_col[s][:], dq[s][:], ACT.Exp, scale=SLOPE).then_inc(cols_exp[s], 1)

            def softmax_row(s, j, row):
                act.wait_ge(rows_ready[s], j * 2 + (row + 1))
                run(M[s][:, 1 - row, :], M[s][:, 1 - row, :], ACT.Exp,
                    scale=(SLOPE - 1.0, 1.0 - SLOPE)[row]).then_inc(rows_exp[s], 1)

            def low_slope(s, j, t):
                if t == 0:
                    act.wait_ge(cols_exp[s], j + 1)
                    act.wait_ge(rows_exp[s], j * 2 + 1)
                if t == 2:
                    act.wait_ge(att_sum[s], j * 3 + 1)
                    act.wait_ge(atl_ready[s], j * 4 + 2)
                run(ATT[s][t], M[s][:, 1, :], scale=b_col[s][:, t:t + 1]).then_inc(btmp_ready[s], 1)

            def split_att(s, j, t):
                if t == 0:
                    act.wait_ge(kv_done[s], j * 4)
                act.wait_ge(att_ready[s], j * 4 + (t + 1))
                run(ATH[s][t], ATT[s][t]).then_inc(ath_ready[s], 1)

            def sum_row(s, j):
                act.wait_ge(rb_done[s], j + 1)
                run(M[s][:, 0, :], psum[s][:, 1, :]).then_inc(rrow_ready[s], 1)

            def relu_rows(s, j):
                for o in range(NT):
                    act.wait_ge(scaled_ready[s], j * 2 + (o + 1))
                    run(M[s][:, 1 + o, :], M[s][:, 1 + o, :], ACT.Relu,
                        bias=bm_col[:, o:o + 1]).then_inc(relu_ready[s], 1)

            def split_xt(s, j, l):
                for h in range(2):
                    act.wait_ge(ht_done[s], j * 4 + (2 * l + h + 1))
                    run(XH[s][:, h, :], psum[s][:, 1 + h, :]).then_inc(hth_ready[s], 1)

            def split_z(s, j, l, kind, part):
                act.wait_ge(z_done[s], j * 8 + (4 * l + 2 * kind + part + 1))
                run(ZS[s][:, 4 * kind + part, :],
                    psum[s][:, (3, 0, 1, 2)[2 * kind + part], :]).then_inc(zh_ready[s], 1)

            def split_v(s, j, l, n):
                act.wait_ge(v_done[s], j * 4 + (2 * l + n + 1))
                run(VH[s][:, n, :], psum[s][:, 2 * n, :]).then_inc(vh_ready[s], 1)

            def sq_row(s, j, l):
                act.wait_ge(bc_done[s], j * 2 + (l + 1))
                run(M[s][:, 3, 0:nodes], psum[s][:, 0, nodes:2 * nodes]).then_inc(sqrow_ready[s], 1)

            def gauss(s, j, l):
                m = halves(M[s][:, 1, :])
                for n in range(NT):
                    act.wait_ge(dist_ready[s], j * 4 + (2 * l + n + 1))
                    run(m[:, n, :], m[:, n, :], ACT.Exp, scale=inv_s2[l][:],
                        bias=gbias[s][:, n:n + 1]).then_inc(gauss_ready[s], 1)

            def split_kt(s, j, l):
                act.wait_ge(kt_done[s], j * 2 + (l + 1))
                run(ZS[s][:, 0, :], psum[s][:, 3, :]).then_inc(kth_ready[s], 1)

            def split_x2(s, j):
                for n in range(NT):
                    act.wait_ge(cur_ready[s], j * 8 + (2 + n + 1))
                    run(XH[s][:, n, :], CUR[s][:, n, :]).then_inc(x2h_ready[s], 1)

            def attention_start(s, j):
                softmax_row(s, j, 0)
                low_slope(s, j, 0)
                softmax_row(s, j, 1)
                low_slope(s, j, 1)
                split_att(s, j, 0)
                split_att(s, j, 1)

            def attention_end(s, j):
                for t in (2, 3):
                    low_slope(s, j, t)
                for t in (2, 3):
                    split_att(s, j, t)

            def start():
                split_x(0, 0)
                prepare(0)
                round_wv(0)
                split_adj_x(0, 0)
                prepare(1)
                gates()
                softmax_columns(0, 0)
                attention_start(0, 0)
                prepare(2, (0, 1))
                attention_end(0, 0)
                prepare(2, (2, 3))
                prepare(3)
                prepare(4)
                round_wv(1)
                prepare(5)
                sum_row(0, 0)
                relu_rows(0, 0)
                prepare(6)
                prepare(7)
                split_xt(0, 0, 0)

            def middle_slot(s, js, l, r, jr):
                sq_row(r, jr, 0)
                gauss(r, jr, 0)
                split_z(s, js, l, 0, 0)
                split_z(s, js, l, 0, 1)
                split_kt(r, jr, 0)
                split_z(s, js, l, 1, 0)
                split_x2(r, jr)
                split_z(s, js, l, 1, 1)
                split_v(s, js, l, 0)
                split_xt(r, jr, 1)
                split_v(s, js, l, 1)

            def seam_slot(s, js, l, r, jr, jn):
                if jr is not None:
                    sq_row(r, jr, 1)
                if jn is not None:
                    split_x(r, jn)
                if jr is not None:
                    gauss(r, jr, 1)
                split_z(s, js, l, 0, 0)
                if jn is not None:
                    split_adj_x(r, jn)
                split_z(s, js, l, 0, 1)
                if jn is not None:
                    softmax_columns(r, jn)
                if jr is not None:
                    split_kt(r, jr, 1)
                if jn is not None:
                    attention_start(r, jn)
                split_z(s, js, l, 1, 0)
                if jn is not None:
                    attention_end(r, jn)
                split_z(s, js, l, 1, 1)
                if jn is not None:
                    sum_row(r, jn)
                    relu_rows(r, jn)
                split_v(s, js, l, 0)
                split_v(s, js, l, 1)
                if jn is not None:
                    split_xt(r, jn, 0)

            def tail(r, j):
                sq_row(r, j, 1)
                gauss(r, j, 1)
                split_kt(r, j, 1)

            start()
            seam_slot(0, 0, 0, 1, None, 0)
            with act.Fori(0, TURNS - 1) as i:
                middle_slot(1, i, 0, 0, i)
                middle_slot(0, i, 1, 1, i)
                seam_slot(1, i, 1, 0, i, i + 1)
                seam_slot(0, i + 1, 0, 1, i, i + 1)
            e = TURNS - 1
            middle_slot(1, e, 0, 0, e)
            middle_slot(0, e, 1, 1, e)
            seam_slot(1, e, 1, 0, e, None)
            tail(1, e)

        @block.vector
        def _(dve):
            tt = nc.vector.tensor_tensor
            ts = nc.vector.tensor_scalar
            stt = nc.vector.scalar_tensor_tensor

            links = [0, 0]

            def own(s, j, ins):
                links[s] += 1
                ins.then_inc(dve_link[s], 1)
                dve.wait_ge(dve_link[s], j * DVE_LINKS + links[s])

            def low(dst, src, hi):
                return tt(dst, src, plain(hi), ALU.subtract)

            prep = [0]

            def link(ins):
                prep[0] += 1
                ins.then_inc(prep_link, 1)
                dve.wait_ge(prep_link, prep[0])

            nc.vector.memset(minus_half[:], -0.5)
            nc.vector.memset(ones[:], 1.0)
            dve.wait_ge(adj_loaded, 16 * 5)
            dve.wait_ge(ident_ready, 1)
            dve.wait_ge(adj_t_done, 1)
            link(nc.vector.tensor_copy(adj_rhs[:, :, 0:nodes],
                                       psum[1][:, 3, :].rearrange("p (t m) -> p t m", m=nodes)))
            link(nc.vector.tensor_copy(adj_rhs_hi[:], adj_rhs))
            low(adj_rhs_lo[:], adj_rhs, adj_rhs_hi[:]).then_inc(adj_prep, 1)

            def prepare_adj():
                nc.vector.tensor_copy(adj_off[:], adj_nat)
                link(tt(w2_full, adj_nat, adj_nat, ALU.mult))
                for t in range(NT):
                    blk = slice(t * P, (t + 1) * P)
                    tt(w2_full[:, t, blk], w2_full[:, t, blk], ident[:], ALU.add)
                    link(tt(scratch[t], adj_nat[:, t, blk], ident[:], ALU.mult))
                    link(tt(adj_off[:, t, blk], adj_nat[:, t, blk], scratch[t], ALU.subtract))
                link(nc.vector.tensor_copy(w2_hi[:], w2_full))
                low(w2_lo[:], w2_full, w2_hi[:])

            def prepare_gates():
                dve.wait_ge(gate_exp, 4)
                for l in range(2):
                    link(ts(gate_tmp[:, l, 1:2], gate_tmp[:, l, 0:1], 1.0, None, ALU.add))
                    link(nc.vector.reciprocal(mix[l][:, 0:1], gate_tmp[:, l, 1:2]))
                    link(ts(mix[l][:, 1:2], mix[l][:, 0:1], -1.0, 1.0, ALU.mult, ALU.add))

            def prepare(q, tiles=range(FT)):
                for t in tiles:
                    dve.wait_ge(prep_hi, 4 * q + t + 1)
                    low(lo_of[jobs[q]][:, t, :], psum[1][:, t, :], hi_of[jobs[q]][:, t, :]).then_inc(prep_out, 1)

            def split_wv(l):
                for h in range(2):
                    dve.wait_ge(wv_rounded, 2 * l + h + 1)
                    part = slice(2 * h, 2 * h + 2)
                    low(wv_lo[:, part, :], nat_b[:, part, :], wv_hi[:, part, :]).then_inc(wv_split, 1)

            def norm_stats(s, j, layer):
                for n in range(NT):
                    dve.wait_ge(res_ready[s], j * 8 + (2 * layer + n + 1))
                    ins = nc.vector.bn_stats(stats[s][:, n, :], CUR[s][:, n, :])
                ins.then_inc(stats_ready[s], 1)
                dve.wait_ge(stats_ready[s], j * 4 + (layer + 1))
                nc.vector.tensor_copy(count[s][:], stats[s][:, 0, 0:1])
                for n in range(NT):
                    ins = nc.vector.bn_aggr(mv[s][:, n, :], stats[s][:, n, :])
                ins.then_inc(mean_ready[s], 1)
                dve.wait_ge(mean_ready[s], j * 4 + (layer + 1))
                ts(veps[s][:], mv[s][:, :, 1], EPS_LN, None, ALU.add).then_inc(var_ready[s], 1)

            def normalise(s, j, layer):
                dve.wait_ge(rstd_ready[s], j * 4 + (layer + 1))
                for n in range(NT):
                    ins = ts(CUR[s][:, n, :], CUR[s][:, n, :], mv[s][:, n, 0:1], rstd[s][:, n:n + 1],
                             ALU.subtract, ALU.mult)
                    ins.then_inc(cur_ready[s], 1)

            def split_adj_x(s, j):
                def lo(n):
                    t = TILE_ORDER[n]
                    dve.wait_ge(yth_ready[s], j * 4 + (n + 1))
                    low(YTL[s][:, t, :], psum[s][:, t, 0:nodes], YTH[s][:, t, :]).then_inc(ytl_ready[s], 1)

                lo(0)
                lo(1)
                dve.wait_ge(yth_ready[s], j * 4 + 4)
                own(s, j, nc.vector.tensor_copy(qk[s][:], psum[s][:, :, nodes:nodes + 2]))
                own(s, j, nc.vector.reduce_max(qmax_col[s][:], qk[s][:, :, 0], AX.X))
                nc.vector.tensor_copy(squares(M[s][:, 2, :]), qk[s][:, :, 1:2].to_broadcast([P, FT, P]))
                nc.vector.tensor_copy(M[s][:, 3, 0:P],
                                      qmax_col[s][:].to_broadcast([P, P])).then_inc(kmat_ready[s], 1)
                lo(2)
                lo(3)

            def softmax_args(s, j):
                dve.wait_ge(kb_done[s], j + 1)
                own(s, j, nc.vector.reduce_max(qmax[s][:], psum[s][:, 1, 0:P], AX.X))
                ts(dq[s][:], qk[s][:, :, 0], qmax[s][:], None, ALU.subtract).then_inc(dq_ready[s], 1)
                ts(M[s][:, 1, :], psum[s][:, 2, :], qmax[s][:], 0.0, ALU.add,
                   ALU.max).then_inc(rows_ready[s], 1)

            def softmax_row(s, j):
                ts(M[s][:, 0, :], psum[s][:, 2, :], qmax[s][:], 0.0, ALU.add,
                   ALU.min).then_inc(rows_ready[s], 1)

            def attention(s, j, t):
                dve.wait_ge(rows_exp[s], j * 2 + 2)
                dve.wait_ge(btmp_ready[s], j * 4 + (t + 1))
                stt(ATT[s][t], M[s][:, 0, :], a_col[s][:, t:t + 1], ATT[s][t],
                    ALU.mult, ALU.max).then_inc(att_ready[s], 1)

            def split_att(s, j, t):
                dve.wait_ge(ath_ready[s], j * 4 + (t + 1))
                low(ATL[s][t], ATT[s][t], ATH[s][t]).then_inc(atl_ready[s], 1)

            def sum_squares(s, j):
                dve.wait_ge(s_done[s], j + 1)
                own(s, j, nc.vector.reciprocal(rsum[s][:], psum[s][:, 2, 0:FT]))
                nc.vector.tensor_copy(squares(M[s][:, 3, :]),
                                      rsum[s][:].unsqueeze(2).to_broadcast([P, FT, P])).then_inc(smat_ready[s], 1)

            def scale_agg(s, j):
                dve.wait_ge(rrow_ready[s], j + 1)
                for o, bank in enumerate((3, 0)):
                    dve.wait_ge(agg_done[s], j * 2 + (o + 1))
                    tt(M[s][:, 1 + o, :], psum[s][:, bank, :], M[s][:, 0, :],
                       ALU.mult).then_inc(scaled_ready[s], 1)

            def add_x(s, j):
                dve.wait_ge(stored[s], j * 16)
                for o in range(NT):
                    dve.wait_ge(relu_ready[s], j * 2 + (o + 1))
                    ins = tt(CUR[s][:, o, :], M[s][:, 1 + o, :], X[s][:, o, :], ALU.add)
                    ins.then_inc(res_ready[s], 1)

            def split_xt(s, j, l):
                for h in range(2):
                    dve.wait_ge(hth_ready[s], j * 4 + (2 * l + h + 1))
                    low(XL[s][:, h, :], psum[s][:, 1 + h, :], XH[s][:, h, :]).then_inc(htl_ready[s], 1)

            def split_z(s, j, l, kind, part):
                dve.wait_ge(zh_ready[s], j * 8 + (4 * l + 2 * kind + part + 1))
                low(ZS[s][:, 4 * kind + 2 + part, :], psum[s][:, (3, 0, 1, 2)[2 * kind + part], :],
                    ZS[s][:, 4 * kind + part, :]).then_inc(zl_ready[s], 1)

            def split_v(s, j, l, n):
                dve.wait_ge(vh_ready[s], j * 4 + (2 * l + n + 1))
                low(VL[s][:, n, :], psum[s][:, 2 * n, :], VH[s][:, n, :]).then_inc(vl_ready[s], 1)

            def squares_l(s, j, l):
                dve.wait_ge(gram_done[s], j * 4 + (2 * l + 1))
                for n in range(NT):
                    ins = nc.vector.tensor_tensor_reduce(
                        squares(M[s][:, 2, :])[:, n, :], psum[s][:, 3, n * (nodes + P):n * (nodes + P) + P], ident[:],
                        1.0, 0.0, ALU.mult, ALU.add, diag[s][:, 0, n:n + 1])
                own(s, j, ins)
                ts(sq_l[s][:], diag[s][:, 0, :], EPS_KERNEL ** 2, None, ALU.max)

            def cosine_start(s):
                stt(halves(M[s][:, 0, :]), halves(psum[s][:, 3, :]), 0.0, adj_off[:], ALU.max,
                    ALU.mult).then_inc(masked_ready[s], 1)

            def gauss_start(s, j, l):
                dve.wait_ge(gram_done[s], j * 4 + (2 * l + 2))
                for n in range(NT):
                    ins = nc.vector.tensor_tensor_reduce(
                        squares(M[s][:, 2, :])[:, 2 + n, :], psum[s][:, 1, n * (nodes + P):n * (nodes + P) + P], ident[:],
                        1.0, 0.0, ALU.mult, ALU.add, diag[s][:, 1, n:n + 1])
                own(s, j, ins)
                own(s, j, ts(rnq[s][:, 1, :], diag[s][:, 1, :], -0.5, None, ALU.mult))
                ts(gbias[s][:], rnq[s][:, 1, :], inv_s2[l][:], None, ALU.mult).then_inc(sq_ready[s], 1)

            def norm_squares(s, j, l):
                dve.wait_ge(rn_ready[s], j * 2 + (l + 1))
                nc.vector.tensor_copy(
                    squares(M[s][:, 2, :]),
                    rnq[s][:].rearrange("p a b -> p (a b)").unsqueeze(2).to_broadcast([P, 4, P])
                ).then_inc(mat_ready[s], 1)

            def kernel_rows(s, j, l):
                dve.wait_ge(sqrow_ready[s], j * 2 + (l + 1))
                for n in range(NT):
                    tt(halves(M[s][:, 1, :])[:, n, :], halves(psum[s][:, 1, :])[:, n, :],
                       M[s][:, 3, 0:nodes], ALU.add).then_inc(dist_ready[s], 1)
                m = halves(M[s][:, 0, :])
                dve.wait_ge(masked_ready[s], j * 2 + (l + 1))
                for n in range(NT):
                    ins = stt(m[:, n, :], psum[s][:, 0, 0:nodes], rnq[s][:, 0, n:n + 1], m[:, n, :],
                              ALU.mult, ALU.mult, accum_out=deg[s][:, 0, n:n + 1])
                ins.then_inc(cos_ready[s], 1)

            def kernel_mix(s, j, l):
                dve.wait_ge(cos_ready[s], j * 2 + (l + 1))
                m, g = halves(M[s][:, 0, :]), halves(M[s][:, 1, :])
                for n in range(NT):
                    dve.wait_ge(gauss_ready[s], j * 4 + (2 * l + n + 1))
                    ins = stt(g[:, n, :], g[:, n, :], 1.0, adj_off[:, n, :], ALU.min, ALU.mult,
                              accum_out=deg[s][:, 1, n:n + 1])
                own(s, j, ins)
                ts(degm[s][:], deg[s][:], EPS_KERNEL, None, ALU.max)
                own(s, j, ts(g, g, mix[l][:, 1:2], None, ALU.mult))
                own(s, j, nc.vector.reciprocal(rdeg[s][:], degm[s][:]))
                own(s, j, stt(coef[s][:], rdeg[s][:, 0, :], mix[l][:, 0:1], degm[s][:, 1, :],
                              ALU.mult, ALU.mult))
                for n in range(NT):
                    ins = stt(m[:, n, :], m[:, n, :], coef[s][:, n:n + 1], g[:, n, :], ALU.mult, ALU.add)
                ins.then_inc(k_ready[s], 1)

            def split_kt(s, j, l):
                dve.wait_ge(kth_ready[s], j * 2 + (l + 1))
                low(ZS[s][:, 1, :], psum[s][:, 3, :], ZS[s][:, 0, :]).then_inc(ktl_ready[s], 1)

            def add_kv(s, j, l, n):
                dve.wait_ge(kv_done[s], j * 4 + (2 * l + n + 1))
                stt(CUR[s][:, n, :], psum[s][:, n, :], rdeg[s][:, 1, n:n + 1], CUR[s][:, n, :],
                    ALU.mult, ALU.add).then_inc(res_ready[s], 1)

            def split_x2(s, j):
                for n in range(NT):
                    dve.wait_ge(x2h_ready[s], j * 2 + (n + 1))
                    low(XL[s][:, n, :], CUR[s][:, n, :], XH[s][:, n, :]).then_inc(x2l_ready[s], 1)

            def add_bias2(s, j):
                for m in range(NT):
                    dve.wait_ge(l2_done[s], j * 2 + (m + 1))
                    tt(CUR[s][:, m, :], psum[s][:, 2 + m, :], bias2_row[:], ALU.add).then_inc(res_ready[s], 1)

            def start():
                prepare_adj()
                prepare(0)
                split_wv(0)
                split_adj_x(0, 0)
                prepare(1)
                softmax_args(0, 0)
                softmax_row(0, 0)
                for t in (0, 2):
                    attention(0, 0, t)
                    attention(0, 0, t + 1)
                    split_att(0, 0, t)
                    split_att(0, 0, t + 1)
                    prepare(2, (t, t + 1))
                prepare(3)
                prepare(4)
                prepare_gates()
                split_wv(1)
                prepare(5)
                sum_squares(0, 0)
                scale_agg(0, 0)
                add_x(0, 0)
                norm_stats(0, 0, 0)
                normalise(0, 0, 0)
                prepare(6)
                prepare(7)
                split_xt(0, 0, 0)

            def middle_slot(s, js, l, r, jr):
                kernel_rows(r, jr, 0)
                kernel_mix(r, jr, 0)
                split_v(r, jr, 0, 1)
                split_z(s, js, l, 0, 0)
                split_z(s, js, l, 0, 1)
                split_kt(r, jr, 0)
                add_kv(r, jr, 0, 0)
                add_kv(r, jr, 0, 1)
                norm_stats(r, jr, 1)
                split_z(s, js, l, 1, 0)
                normalise(r, jr, 1)
                split_x2(r, jr)
                split_z(s, js, l, 1, 1)
                squares_l(s, js, l)
                add_bias2(r, jr)
                norm_stats(r, jr, 2)
                normalise(r, jr, 2)
                gauss_start(s, js, l)
                split_v(s, js, l, 0)
                norm_squares(s, js, l)
                cosine_start(s)
                split_xt(r, jr, 1)
                if s == 0:
                    split_v(s, js, l, 1)

            def seam_slot(s, js, l, r, jr, jn):
                if jr is not None:
                    kernel_rows(r, jr, 1)
                    kernel_mix(r, jr, 1)
                split_z(s, js, l, 0, 0)
                if jn is not None:
                    end_batch_links(r)
                    split_adj_x(r, jn)
                split_z(s, js, l, 0, 1)
                if jn is not None:
                    softmax_args(r, jn)
                if jr is not None:
                    split_kt(r, jr, 1)
                if jn is not None:
                    softmax_row(r, jn)
                if jr is not None:
                    add_kv(r, jr, 1, 0)
                if jn is not None:
                    attention(r, jn, 0)
                    attention(r, jn, 1)
                if jr is not None:
                    add_kv(r, jr, 1, 1)
                if jn is not None:
                    split_att(r, jn, 0)
                    split_att(r, jn, 1)
                split_z(s, js, l, 1, 0)
                if jr is not None:
                    norm_stats(r, jr, 3)
                if jn is not None:
                    attention(r, jn, 2)
                    attention(r, jn, 3)
                    split_att(r, jn, 2)
                    split_att(r, jn, 3)
                if jr is not None:
                    normalise(r, jr, 3)
                split_z(s, js, l, 1, 1)
                if jn is not None:
                    sum_squares(r, jn)
                    scale_agg(r, jn)
                squares_l(s, js, l)
                if jn is not None:
                    add_x(r, jn)
                    norm_stats(r, jn, 0)
                gauss_start(s, js, l)
                if jn is not None:
                    normalise(r, jn, 0)
                split_v(s, js, l, 0)
                norm_squares(s, js, l)
                cosine_start(s)
                if jn is not None:
                    split_xt(r, jn, 0)
                if s == 1:
                    split_v(s, js, l, 1)

            def end_batch_links(s):
                assert links[s] in (0, DVE_LINKS), links
                links[s] = 0

            def tail(r, j):
                kernel_rows(r, j, 1)
                kernel_mix(r, j, 1)
                split_kt(r, j, 1)
                add_kv(r, j, 1, 0)
                add_kv(r, j, 1, 1)
                norm_stats(r, j, 3)
                normalise(r, j, 3)

            start()
            seam_slot(0, 0, 0, 1, None, 0)
            with dve.Fori(0, TURNS - 1) as i:
                middle_slot(1, i, 0, 0, i)
                middle_slot(0, i, 1, 1, i)
                seam_slot(1, i, 1, 0, i, i + 1)
                seam_slot(0, i + 1, 0, 1, i, i + 1)
            e = TURNS - 1
            middle_slot(1, e, 0, 0, e)
            middle_slot(0, e, 1, 1, e)
            seam_slot(1, e, 1, 0, e, None)
            tail(1, e)

        @block.gpsimd
        def _(pool):
            nc.gpsimd.memset(ident[:], 0.0).then_inc(zeros_ready, 1)
            pool.wait_ge(zeros_ready, 1)
            nc.gpsimd.affine_select(out=ident[:], in_=ident[:], compare_op=ALU.not_equal, fill=1.0, base=0,
                                    pattern=[[-1, P]], channel_multiplier=1).then_inc(ident_ready, 1)

            def split_x(s, j):
                pool.wait_ge(xh_ready[s], j + 1)
                nc.gpsimd.tensor_tensor(XL[s], X[s], plain(XH[s]), ALU.subtract).then_inc(xl_ready[s], 1)

            def add_att(s, j, tiles):
                pool.wait_ge(atl_ready[s], j * 4 + 1)
                for t in tiles:
                    pool.wait_ge(att_ready[s], j * 4 + (t + 1))
                    if t > 1:
                        pool.wait_ge(att_sum[s], j * 3 + (t - 1))
                    nc.gpsimd.tensor_tensor(ATT[s][0], ATT[s][0], ATT[s][t], ALU.add).then_inc(att_sum[s], 1)

            def inverse_std(s, j, layer):
                pool.wait_ge(var_ready[s], j * 4 + (layer + 1))
                nc.gpsimd.tensor_tensor(rstd[s][:], veps[s][:], minus_half[:], ALU.pow).then_inc(rstd_ready[s], 1)

            def inverse_norm(s, j, l):
                pool.wait_ge(sq_ready[s], j * 2 + (l + 1))
                nc.gpsimd.tensor_tensor(rnq[s][:, 0, :], sq_l[s][:], minus_half[:],
                                        ALU.pow).then_inc(rn_ready[s], 1)

            def middle_slot(s, js, l, r, jr):
                inverse_std(r, jr, 1)
                inverse_std(r, jr, 2)
                inverse_norm(s, js, l)

            def seam_slot(s, js, l, r, jr, jn):
                if jn is not None:
                    split_x(r, jn)
                if jn is not None:
                    add_att(r, jn, (1,))
                if jr is not None:
                    inverse_std(r, jr, 3)
                if jn is not None:
                    add_att(r, jn, (2, 3))
                    inverse_std(r, jn, 0)
                inverse_norm(s, js, l)

            split_x(0, 0)
            add_att(0, 0, (1, 2, 3))
            inverse_std(0, 0, 0)
            seam_slot(0, 0, 0, 1, None, 0)
            with pool.Fori(0, TURNS - 1) as i:
                middle_slot(1, i, 0, 0, i)
                middle_slot(0, i, 1, 1, i)
                seam_slot(1, i, 1, 0, i, i + 1)
                seam_slot(0, i + 1, 0, 1, i, i + 1)
            e = TURNS - 1
            middle_slot(1, e, 0, 0, e)
            middle_slot(0, e, 1, 1, e)
            seam_slot(1, e, 1, 0, e, None)
            inverse_std(1, e, 3)


_INS = ["x", "adj", "L0_gnn_wq", "L0_gnn_wk", "L0_gnn_bm",
        "L1_gnn_W_lang", "L1_gnn_W_grav", "L1_gnn_W_V", "L1_gnn_W_O", "L1_gnn_gate_logit", "L1_gnn_log_sigma",
        "L2_gnn_bias",
        "L3_gnn_W_lang", "L3_gnn_W_grav", "L3_gnn_W_V", "L3_gnn_W_O", "L3_gnn_gate_logit", "L3_gnn_log_sigma"]
_OUTS = [((32, 256, 512), "float32")]


def kernel(**inputs):
    import numpy as _np
    import concourse.bacc as _bacc
    from concourse import mybir as _mybir
    from concourse.bass_utils import run_bass_kernel_spmd as _run

    nc = _bacc.Bacc("TRN2", target_bir_lowering=False, num_devices=1)
    arrays, args = {}, []
    for name in _INS:
        a = _np.ascontiguousarray(inputs[name])
        if a.ndim == 0:
            a = a.reshape(1)
        arrays[f"in_{name}_dram"] = a
        args.append(nc.dram_tensor(f"in_{name}_dram", a.shape, _mybir.dt.from_np(a.dtype), kind="ExternalInput").ap())
    for i, (shape, dtype) in enumerate(_OUTS):
        dt = _mybir.dt.from_np(_np.dtype(dtype))
        args.append(nc.dram_tensor(f"out_{i}_dram", shape, dt, kind="ExternalOutput").ap())
    gnn_stack(nc, *args)
    r = _run(nc, [arrays], core_ids=[0])
    return r.results[0]["out_0_dram"]
```
